# Optimizing a Trainium2 kernel written in Bass

```python
import numpy as np
import jax
import jax.numpy as jnp

def _softmax(x, axis=-1):
    return jax.nn.softmax(x, axis=axis)

def _gelu(x):
    return jax.nn.gelu(x, approximate=True)

def _silu(x):
    return jax.nn.silu(x)

def _sigmoid(x):
    return jax.nn.sigmoid(x)

def _layernorm(x, axis=-1, eps=1e-05):
    m = jnp.mean(x, axis=axis, keepdims=True)
    v = jnp.var(x, axis=axis, keepdims=True)
    return (x - m) / jnp.sqrt(v + eps)

def _scatter_add(tgt, idx, src, axis=0):
    return tgt.at[idx].add(src)

def _segment_sum(src, seg, n):
    return jax.ops.segment_sum(src, seg, n)
kernel_name = 'mk_hybrid_d1_jaxref_r4_9cb5f9'

def setup_inputs(seed: int=0):
    np.random.seed(seed)
    _w = jnp.asarray

    def _L0_attn_a_setup():
        import jax, jax.numpy as jnp
        import numpy as np
        B, T, E = (4, 512, 256)
        H = 16
        D = E // H
        key = jax.random.key(seed)
        k1, k2, k3 = jax.random.split(key, 3)
        x = jax.random.normal(k1, (B, T, E), dtype=jnp.float32)
        W_qkv = jax.random.normal(k2, (3 * E, E), dtype=jnp.float32) * E ** (-0.5)
        W_out = jax.random.normal(k3, (E, E), dtype=jnp.float32) * E ** (-0.5)
        return {'x': x, 'W_qkv': W_qkv, 'W_out': W_out}
    _L0_attn_a_in = _L0_attn_a_setup()

    def _L0_attn_b_setup():
        import jax, jax.numpy as jnp
        import numpy as np
        H = 16
        G = 4
        THETA = 10000.0

        def _rope(x, cos, sin):
            x0 = x[..., ::2]
            x1 = x[..., 1::2]
            r0 = x0 * cos - x1 * sin
            r1 = x0 * sin + x1 * cos
            return jnp.stack([r0, r1], axis=-1).reshape(x.shape)
        key = jax.random.key(seed)
        ks = jax.random.split(key, 5)
        B, S, D = (2, 512, 256)
        return {'x': jax.random.normal(ks[0], (B, S, D), jnp.float32), 'Wq': jax.random.normal(ks[1], (D, D), jnp.float32) * 0.02, 'Wk': jax.random.normal(ks[2], (D, D // G), jnp.float32) * 0.02, 'Wv': jax.random.normal(ks[3], (D, D // G), jnp.float32) * 0.02, 'Wo': jax.random.normal(ks[4], (D, D), jnp.float32) * 0.02}
    _L0_attn_b_in = _L0_attn_b_setup()

    def _L0_ffn_setup():
        import jax, jax.numpy as jnp
        import numpy as np
        INT4_QMAX = 7.0

        def simulate_quantize_int4(w):
            scale = jnp.max(jnp.abs(w)) / INT4_QMAX
            q = jnp.clip(jnp.round(w / scale), -8.0, 7.0)
            return q * scale
        key = jax.random.key(seed)
        k_x, k_w, k_bias, k_a, k_b = jax.random.split(key, 5)
        d_in, features, rank = (256, 256, 16)
        x = jax.random.normal(k_x, (4, 2048, d_in), dtype=jnp.float32)
        kernel = jax.random.normal(k_w, (d_in, features), dtype=jnp.float32)
        bias = jax.random.normal(k_bias, (features,), dtype=jnp.float32)
        a = jax.random.normal(k_a, (d_in, rank), dtype=jnp.float32) * (1.0 / np.sqrt(d_in))
        b = jax.random.normal(k_b, (rank, features), dtype=jnp.float32) * 0.01
        return {'x': x, 'kernel': kernel, 'bias': bias, 'a': a, 'b': b}
    _L0_ffn_in = _L0_ffn_setup()
    _d = {'L0_attn_a_x': _L0_attn_a_in['x'], 'L0_attn_a_W_qkv': _L0_attn_a_in['W_qkv'], 'L0_attn_a_W_out': _L0_attn_a_in['W_out'], 'L0_attn_b_Wq': _L0_attn_b_in['Wq'], 'L0_attn_b_Wk': _L0_attn_b_in['Wk'], 'L0_attn_b_Wv': _L0_attn_b_in['Wv'], 'L0_attn_b_Wo': _L0_attn_b_in['Wo'], 'L0_ffn_kernel': _L0_ffn_in['kernel'], 'L0_ffn_bias': _L0_ffn_in['bias'], 'L0_ffn_a': _L0_ffn_in['a'], 'L0_ffn_b': _L0_ffn_in['b']}
    _x0 = _d['L0_attn_a_x']
    _d['L0_attn_a_x'] = jax.random.normal(jax.random.fold_in(jax.random.key(seed), 1), (16, 1024, 256), dtype=_x0.dtype)
    del _x0
    return _d

def reference(L0_attn_a_x, L0_attn_a_W_qkv, L0_attn_a_W_out, L0_attn_b_Wq, L0_attn_b_Wk, L0_attn_b_Wv, L0_attn_b_Wo, L0_ffn_kernel, L0_ffn_bias, L0_ffn_a, L0_ffn_b):

    def _L0_attn_a_ref(x, W_qkv, W_out):
        import jax, jax.numpy as jnp
        import numpy as np
        B, T, E = (4, 512, 256)
        H = 16
        D = E // H
        b, t, c = x.shape
        scale = D ** (-0.5)
        qkv = jnp.einsum('btc,fc->btf', x, W_qkv)
        q, k, v = jnp.split(qkv, 3, axis=-1)
        q = q.reshape(b, t, H, D).transpose(0, 2, 1, 3)
        k = k.reshape(b, t, H, D).transpose(0, 2, 1, 3)
        v = v.reshape(b, t, H, D).transpose(0, 2, 1, 3)
        attn = jnp.einsum('bhqd,bhkd->bhqk', q, k) * scale
        causal = jnp.triu(jnp.ones((t, t), dtype=bool), k=1)
        attn = jnp.where(causal, -jnp.inf, attn)
        attn = jax.nn.softmax(attn, axis=-1)
        out = jnp.einsum('bhqk,bhkd->bhqd', attn, v)
        out = out.transpose(0, 2, 1, 3).reshape(b, t, c)
        return jnp.einsum('btc,oc->bto', out, W_out)

    def _L0_attn_b_ref(x, Wq, Wk, Wv, Wo):
        import jax, jax.numpy as jnp
        import numpy as np
        H = 16
        G = 4
        THETA = 10000.0

        def _rope(x, cos, sin):
            x0 = x[..., ::2]
            x1 = x[..., 1::2]
            r0 = x0 * cos - x1 * sin
            r1 = x0 * sin + x1 * cos
            return jnp.stack([r0, r1], axis=-1).reshape(x.shape)
        B, S, D = x.shape
        hd = D // H
        Hkv = H // G
        q = x @ Wq
        k = x @ Wk
        v = x @ Wv
        k = jnp.repeat(k.reshape(B, S, Hkv, hd), G, axis=2)
        v = jnp.repeat(v.reshape(B, S, Hkv, hd), G, axis=2)
        inv = 1.0 / THETA ** (jnp.arange(0, D, 2, dtype=jnp.float32) / D)
        ang = jnp.arange(S, dtype=jnp.float32)[:, None] * inv[None, :]
        q = _rope(q, jnp.cos(ang)[None], jnp.sin(ang)[None])
        angk = ang[:, :hd // 2]
        k = _rope(k, jnp.cos(angk)[None, :, None, :], jnp.sin(angk)[None, :, None, :])
        q = q.reshape(B, S, H, hd).transpose(0, 2, 1, 3)
        k = k.transpose(0, 2, 1, 3)
        v = v.transpose(0, 2, 1, 3)
        scores = jnp.einsum('bhqd,bhkd->bhqk', q, k) / jnp.sqrt(jnp.float32(D))
        p = jax.nn.softmax(scores, axis=-1)
        o = jnp.einsum('bhqk,bhkd->bhqd', p, v)
        o = o.transpose(0, 2, 1, 3).reshape(B, S, D)
        return o @ Wo

    def _L0_ffn_ref(x, kernel, bias, a, b):
        import jax, jax.numpy as jnp
        import numpy as np
        INT4_QMAX = 7.0

        def simulate_quantize_int4(w):
            scale = jnp.max(jnp.abs(w)) / INT4_QMAX
            q = jnp.clip(jnp.round(w / scale), -8.0, 7.0)
            return q * scale
        w = simulate_quantize_int4(kernel)
        y = jnp.einsum('bsd,df->bsf', x, w) + bias
        lora = jnp.einsum('bsr,rf->bsf', jnp.einsum('bsd,dr->bsr', x, a), b)
        return y + lora
    x = L0_attn_a_x
    x = x + _L0_attn_a_ref(_layernorm(x, axis=-1), L0_attn_a_W_qkv, L0_attn_a_W_out)
    x = x + _L0_ffn_ref(_layernorm(x, axis=-1), L0_ffn_kernel, L0_ffn_bias, L0_ffn_a, L0_ffn_b)
    x = x + _L0_attn_b_ref(_layernorm(x, axis=-1), L0_attn_b_Wq, L0_attn_b_Wk, L0_attn_b_Wv, L0_attn_b_Wo)
    x = x + _L0_ffn_ref(_layernorm(x, axis=-1), L0_ffn_kernel, L0_ffn_bias, L0_ffn_a, L0_ffn_b)
    return x

_drawn_inputs = setup_inputs


def setup_inputs(seed=0):
    import zlib

    import numpy as np

    out = dict(_drawn_inputs(seed))
    spreads = {}
    factors = {'L0_attn_b_Wq': 8.0,
     'L0_attn_b_Wk': 8.0,
     'L0_attn_b_Wv': 8.0,
     'L0_attn_b_Wo': 8.0,
     'L0_ffn_a': 8.0,
     'L0_ffn_b': 8.0}
    for name, (base, spread) in spreads.items():
        noise = np.random.default_rng([zlib.crc32(name.encode()), seed]).standard_normal(out[name].shape)
        drawn = base * np.exp(spread * noise) if base else spread * noise
        out[name] = jnp.asarray(drawn.astype(out[name].dtype))
    for name, factor in factors.items():
        out[name] = (out[name] * factor).astype(out[name].dtype)
    return out
```

```python
from contextlib import ExitStack

import numpy as np
import concourse.bass as bass
from concourse import mybir

F32 = mybir.dt.float32
BF16 = mybir.dt.bfloat16
ALU = mybir.AluOpType
ACT = mybir.ActivationFunctionType
AX = mybir.AxisListType

P = 128
BATCH, T, E = 16, 1024, 256
H, D = 16, 16
G = 4
NG = H // G
NT = T // P
BANK = 512
EC = E // P
SUB = BANK // P
TILES = BATCH * T // BANK
PARTS = 3
SPLIT = 6 * D
ROWS = SPLIT + 2
Q_PARTS = (0, 0, 0, 1, 1, 2)
K_PARTS = (0, 1, 2, 0, 1, 0)
HIDDEN = -1.0e30
EPS = 1e-5
QMAX = 7.0
ROUND = 12582912.0
LORA = 16


def wait(eng, sem, value):
    if not isinstance(value, int) or value > 0:
        eng.wait_ge(sem, value)


def apart(eng, spare):
    eng.sem_inc(spare, 1)


def weights_phase(nc, src, w, const):
    with ExitStack() as ctx:
        sb = lambda name, shape, dt=F32: ctx.enter_context(nc.sbuf_tensor(name, shape, dt))
        sem = lambda name: ctx.enter_context(nc.semaphore(name))
        ffn_raw = sb("ffn_raw", [P, EC, E])
        lora_aT = sb("lora_aT", [LORA, E])
        lora_b = sb("lora_b", [LORA, E])
        abs_max = sb("abs_max", [P, 1])
        all_max = sb("all_max", [P, 1])
        scale = sb("scale", [P, 1])
        per_scale = sb("per_scale", [P, 1])
        quant = sb("quant", [P, EC, E])
        lora = ctx.enter_context(nc.psum_tensor("lora", [P, EC, E], F32))
        loaded, ffn_loaded, lora_loaded = sem("weights_loaded"), sem("ffn_loaded"), sem("lora_loaded")
        zeroed, built, rowmax, allmax = sem("zeroed"), sem("masks_built"), sem("row_max"), sem("core_max")
        step, lora_done = sem("quant_step"), sem("lora_done")

        with nc.Block() as block:
            @block.sync
            def _(sp):
                sp.dma_start(ffn_raw[:, :, :], src["ffn"].rearrange("(c p) n -> p c n", p=P)).then_inc(ffn_loaded, 16)
                sp.dma_start(lora_aT[:, :], src["lora_aT"]).then_inc(lora_loaded, 16)
                sp.dma_start(lora_b[:, :], src["lora_b"]).then_inc(lora_loaded, 16)
                count = 0
                for name in ("qkvT", "outT", "q_b", "k_b", "v_b", "out_b"):
                    sp.dma_start(w[name][:, :, :], src[name].rearrange("(c p) n -> p c n", p=P)).then_inc(loaded, 16)
                    count += 16
                bias = src["bias"].rearrange("(a n) -> a n", a=1)
                sp.dma_start(w["bias"][:, 0, :], bias.broadcast_to([P, E])).then_inc(loaded, 16)
                for s in range(1, SUB):
                    sp.dma_start(w["bias"][:, s, :], bias.broadcast_to([P, E])).then_inc(loaded, 16)
                count += 16 * SUB
                sp.wait_ge(loaded, count)

            @block.gpsimd
            def _(pool):
                nc.gpsimd.memset(const["eps"][:, :], EPS).then_inc(built, 1)
                for m in ("ident", "ident16", "hide_qk", "hide_kq"):
                    nc.gpsimd.memset(const[m][:, :], 0.0).then_inc(zeroed, 1)
                pool.wait_ge(zeroed, 4)
                for m in ("ident", "ident16"):
                    nc.gpsimd.affine_select(out=const[m][:, :], in_=const[m][:, :], compare_op=ALU.not_equal,
                                            fill=1.0, base=0, pattern=[[-1, P]], channel_multiplier=1)\
                        .then_inc(built, 1)
                nc.gpsimd.affine_select(out=const["hide_qk"][:, :], in_=const["hide_qk"][:, :],
                                        compare_op=ALU.is_ge, fill=HIDDEN, base=0, pattern=[[-1, P]],
                                        channel_multiplier=1).then_inc(built, 1)
                nc.gpsimd.affine_select(out=const["hide_kq"][:, :], in_=const["hide_kq"][:, :],
                                        compare_op=ALU.is_ge, fill=HIDDEN, base=0, pattern=[[1, P]],
                                        channel_multiplier=-1).then_inc(built, 1)
                pool.wait_ge(built, 5)
                pool.wait_ge(rowmax, 1)
                nc.gpsimd.partition_all_reduce(all_max[:, :], abs_max[:, :], P,
                                               bass.bass_isa.ReduceOp.max).then_inc(allmax, 1)

            @block.tensor
            def _(pe):
                pe.wait_ge(lora_loaded, 32)
                for c in range(EC):
                    mm = nc.tensor.matmul(lora[:, c, :], lora_aT[:, c * P:(c + 1) * P], lora_b[:, :],
                                          start=True, stop=True)
                mm.then_inc(lora_done, 1)

            @block.vector
            def _(dve):
                done = [0]

                def then(ins):
                    done[0] += 1
                    ins.then_inc(step, 1)
                    dve.wait_ge(step, done[0])

                dve.wait_ge(ffn_loaded, 16)
                nc.vector.tensor_reduce(abs_max[:, :], ffn_raw[:, :, :], AX.XY, ALU.max,
                                        apply_absolute_value=True).then_inc(rowmax, 1)
                dve.wait_ge(allmax, 1)
                then(nc.vector.tensor_scalar(scale[:, :], all_max[:, :], 1.0 / QMAX, None, ALU.mult))
                then(nc.vector.reciprocal(per_scale[:, :], scale[:, :]))
                then(nc.vector.tensor_scalar(quant[:, :, :], ffn_raw[:, :, :], per_scale[:, 0:1], ROUND,
                                             ALU.mult, ALU.add))
                then(nc.vector.tensor_scalar(quant[:, :, :], quant[:, :, :], ROUND, -8.0, ALU.subtract, ALU.max))
                then(nc.vector.tensor_scalar(quant[:, :, :], quant[:, :, :], QMAX, scale[:, 0:1], ALU.min, ALU.mult))
                dve.wait_ge(lora_done, 1)
                then(nc.vector.tensor_tensor(w["ffn"][:, :, :], lora[:, :, :], quant[:, :, :], ALU.add))


def token_phase(nc, tag, w, const, x_in, x_out, attended, recip_scr, out_w, qkv, q_scr, k_scr, v_scr, tables):
    ffn = attended is not None
    stages = (["R", "O"] if ffn else ["O"]) + ["A"] + (["F"] if ffn else []) + (["Q"] if qkv else [])
    off = {s: n for n, s in enumerate(stages)}
    chunks = {"a": [("q", 0), ("q", 1), ("k", 0), ("k", 1)], "b": [("q", 0), ("q", 1), ("k", 0)], None: []}[qkv]
    NC = len(chunks)
    V_USES = 2 if qkv == "a" else 1
    USES = NC + V_USES
    KW = {"a": P, "b": E // G, None: P}[qkv]
    VW = E if qkv == "a" else E // G
    VG = VW // NG
    W_Q, W_K, W_V = {"a": (w["qkvT"][:, :, 0:E], w["qkvT"][:, :, E:2 * E], w["qkvT"][:, :, 2 * E:3 * E]),
                     "b": (w["q_b"], w["k_b"], w["v_b"]), None: (None,) * 3}[qkv]

    with ExitStack() as ctx:
        sb = lambda name, shape, dt=F32: ctx.enter_context(nc.sbuf_tensor(tag + name, shape, dt))
        ps = lambda name, shape: ctx.enter_context(nc.psum_tensor(tag + name, shape, F32))
        sem = lambda name: ctx.enter_context(nc.semaphore(tag + name))
        two = lambda make, name, *a: [make(f"{name}{i}", *a) for i in range(2)]

        x_tile = two(sb, "x_tile", [P, SUB, E])
        normed = two(sb, "normed", [P, SUB, E])
        stats = sb("stats", [P, SUB, 6])
        moments = sb("moments", [P, SUB, 2])
        std = sb("std", [P, SUB])
        rstd = sb("rstd", [P, SUB])
        flipped = ps("flipped", [P, EC, BANK])
        if ffn:
            sums = two(sb, "sums", [P, BANK // 8])
            recip = two(sb, "recip", [P, BANK // 8])
            att = two(sb, "att", [P, EC, BANK])
            recip_wide = two(sb, "recip_wide", [P, EC, BANK])
            x1 = two(sb, "x1_", [P, SUB, E])
            x1_bias = two(sb, "x1_bias", [P, SUB, E])
            x2 = two(sb, "x2_", [P, SUB, E])
            ln_f = two(sb, "ln_f", [P, SUB, E])
            flip_f = sb("flip_f", [P, EC, BANK])
            y_att = ps("y_att", [P, SUB, E])
            y_ffn = ps("y_ffn", [P, SUB, E])
        if qkv:
            flip_q = sb("flip_q", [P, EC, BANK])
            part = [[sb(f"part{c}_{k}", [P, BANK], BF16) for k in range(PARTS)] for c in range(NC)]
            rest = [sb(f"rest{c}", [P, BANK]) for c in range(NC)]
            v_tile = sb("v_tile", [P, NG, SUB, VG])
            proj = two(ps, "proj", [P, BANK])
        if qkv == "b":
            cos = {"q": sb("cos_q", [P, EC, T]), "k": sb("cos_k", [KW, 1, T])}
            sin = {"q": sb("sin_q", [P, EC, T]), "k": sb("sin_k", [KW, 1, T])}
            swapped = [sb(f"swapped{c}", [P, BANK]) for c in range(NC)]
            turned = [sb(f"turned{c}", [P, BANK]) for c in range(NC)]

        x_loaded, ln_a_ready = two(sem, "x_loaded"), sem("ln_a_ready")
        ln_step, std_ready = sem("ln_step"), sem("std_ready")
        if ffn:
            sums_loaded, recip_ready, recip_stored = two(sem, "sums_loaded"), sem("recip_ready"), two(sem, "recip_stored")
            att_loaded, att_ready, y_att_ready = two(sem, "att_loaded"), sem("att_ready"), sem("y_att_ready")
            x1_ready, x1_bias_ready = sem("x1_ready"), sem("x1_bias_ready")
            flip_f_ready, flip_f_copied, y_ffn_ready = sem("flip_f_ready"), sem("flip_f_copied"), sem("y_ffn_ready")
            x2_ready, x2_stored = sem("x2_ready"), two(sem, "x2_stored")
        if ffn and qkv:
            ln_f_ready = sem("ln_f_ready")
        if qkv:
            flip_q_ready, flip_q_copied = sem("flip_q_ready"), sem("flip_q_copied")
            proj_ready, high_ready, rest_ready, mid_ready, low_ready = (sem(n) for n in (
                "proj_ready", "high_ready", "rest_ready", "mid_ready", "low_ready"))
            parts_stored = [sem(f"parts_stored{c}") for c in range(NC)]
            v_copied, v_stored = sem("v_copied"), sem("v_stored")
        if qkv == "b":
            swap_ready, cos_ready = sem("swap_ready"), sem("cos_ready")
            turn_step, turned_ready, tables_loaded = sem("turn_step"), sem("turned_ready"), sem("tables_loaded")

        def rounds(eng, body, ahead=0):
            first = 3
            for i in range(2 * first):
                body(i, i // 2, i % 2)
            with eng.Fori(first, TILES // 2 - ahead) as n:
                for u in range(2):
                    body(2 * n + u, n, u)
            for i in range(TILES - 2 * ahead, TILES + len(stages) - 1):
                body(i, i // 2, i % 2)

        def at(stage, i, n, u, ahead=0):
            if stage not in off:
                return None
            d = off[stage] - ahead
            t = i - d
            if isinstance(i, int) and not 0 <= t < TILES:
                return None
            return t, n + (u - d) // 2, (u - d) % 2

        def norms_before(stage, t):
            if not (qkv and ffn):
                return t
            if stage == "A":
                return t + (max(t - 1, 0) if isinstance(t, int) else t - 1)
            return t + (min(t + 2, TILES) if isinstance(t, int) else t + 2)

        with nc.Block() as block:
            @block.sync
            def _(sp):
                def load_sums(t, b, half):
                    wait(sp, recip_ready, t - 1)
                    apart(sp, const["spare"])
                    rows = attended[bass.ds(b * NG * P, NG * P), half * BANK:(half + 1) * BANK]
                    sp.dma_start(sums[half][:, :], rows.rearrange("(h r) (c t) -> h r c t", r=32, c=8)[:, D, :, :])\
                        .then_inc(sums_loaded[half], 16)

                def load_x(t, b, half):
                    wait(sp, x1_ready if ffn else ln_a_ready, t - 1)
                    apart(sp, const["spare"])
                    sp.dma_start(x_tile[half][:, :, :],
                                 x_in[bass.ds(b * T + half * BANK, BANK), :].rearrange("(s p) e -> p s e", p=P))\
                        .then_inc(x_loaded[half], 16)

                def load_attended(t, b, half):
                    wait(sp, y_att_ready, t - 1)
                    apart(sp, const["spare"])
                    for c in range(EC):
                        src = attended[bass.ds((b * NG + 2 * c) * P, 2 * P), half * BANK:(half + 1) * BANK]
                        sp.dma_start(att[half][:, c, :], src.rearrange("(h r) t -> h r t", r=32)[:, 0:D, :])\
                            .then_inc(att_loaded[half], 16)
                    sp.wait_ge(recip_ready, t + 1)
                    apart(sp, const["spare"])
                    sp.dma_start(recip_scr[bass.ds(b * H, H), half * BANK:(half + 1) * BANK]
                                 .rearrange("h (c t) -> h c t", c=8), recip[half][:, :])\
                        .then_inc(recip_stored[half], 16)
                    sp.wait_ge(recip_stored[half], (b + 1) * 16)
                    apart(sp, const["spare"])
                    for c in range(EC):
                        src = recip_scr[bass.ds(b * H + 8 * c, 8), half * BANK:(half + 1) * BANK]
                        sp.dma_start(recip_wide[half][:, c, :],
                                     src.rearrange("h (a t) -> h a t", a=1).broadcast_to([8, D, BANK]))\
                            .then_inc(att_loaded[half], 16)

                def store_x(t, b, half):
                    sp.wait_ge(x2_ready, t + 1)
                    apart(sp, const["spare"])
                    sp.dma_start(x_out[bass.ds(b * T + half * BANK, BANK), :].rearrange("(s p) e -> p s e", p=P),
                                 x2[half][:, :, :]).then_inc(x2_stored[half], 16)

                def store_parts(t, b, half):
                    for c, (kind, at_c) in enumerate(chunks):
                        rows = P if kind == "q" else KW
                        scr = q_scr if kind == "q" else k_scr
                        width = E if kind == "q" or qkv == "a" else KW
                        for k, (ready, count) in enumerate(((high_ready, NC * t + c + 1), (mid_ready, NC * t + c + 1),
                                                            (low_ready, NC * t + c + 1))):
                            sp.wait_ge(ready, count)
                            apart(sp, const["spare"])
                            sp.dma_start(scr[bass.ds((b * PARTS + k) * width + at_c * P, rows),
                                             half * BANK:(half + 1) * BANK], part[c][k][0:rows, :])\
                                .then_inc(parts_stored[c], 16)
                    sp.wait_ge(v_copied, V_USES * (t + 1))
                    apart(sp, const["spare"])
                    for g in range(NG):
                        sp.dma_start(v_scr[bass.ds((b * NG + g) * P, P), half * SUB * VG:(half + 1) * SUB * VG],
                                     v_tile[:, g, :, :].rearrange("p s v -> p (s v)")).then_inc(v_stored, 16)

                if qkv == "b":
                    for name, dst in (("cos_q", cos["q"]), ("sin_q", sin["q"]), ("cos_k", cos["k"]), ("sin_k", sin["k"])):
                        sp.dma_start(dst[:, :, :], tables[name].rearrange("(c p) t -> p c t", p=dst.shape[0]))\
                            .then_inc(tables_loaded, 16)
                if ffn:
                    load_sums(0, 0, 0)
                else:
                    load_x(0, 0, 0)

                def body(i, n, u):
                    if at("R", i, n, u, 1):
                        load_sums(*at("R", i, n, u, 1))
                    if at("R", i, n, u):
                        load_attended(*at("R", i, n, u))
                    if at("O", i, n, u, 0 if ffn else 1):
                        load_x(*at("O", i, n, u, 0 if ffn else 1))
                    if at("F", i, n, u):
                        store_x(*at("F", i, n, u))
                    if at("Q", i, n, u):
                        store_parts(*at("Q", i, n, u))

                rounds(sp, body, 1)
                if ffn:
                    for half in range(2):
                        sp.wait_ge(x2_stored[half], 16 * BATCH)
                if qkv:
                    for c in range(NC):
                        sp.wait_ge(parts_stored[c], 16 * PARTS * TILES)
                    sp.wait_ge(v_stored, 16 * NG * TILES)
                    apart(sp, const["spare"])

            @block.tensor
            def _(pe):
                def turn(src, ready):
                    for c in range(EC):
                        for s in range(SUB):
                            mm = nc.tensor.transpose(flipped[:, c, s * P:(s + 1) * P],
                                                     src[:, s, c * P:(c + 1) * P], const["ident"][:, :])
                    mm.then_inc(ready, 1)

                def rows_times(dst, lhs, rhs, ready):
                    for s in range(SUB):
                        for c in range(EC):
                            mm = nc.tensor.matmul(dst[:, s, :], lhs[:, c, s * P:(s + 1) * P], rhs[:, c, :],
                                                  start=(c == 0), stop=(c == EC - 1))
                    mm.then_inc(ready, 1)

                def flip_for_ffn(t, b, half):
                    pe.wait_ge(ln_a_ready, t + 1)
                    if "Q" in off:
                        wait(pe, flip_q_copied, t - 1)
                    else:
                        wait(pe, flip_f_copied, t)
                    turn(normed[half], flip_f_ready)

                def out_projection(t, b, half):
                    pe.wait_ge(att_ready, t + 1)
                    wait(pe, x1_ready, t)
                    rows_times(y_att, att[half], out_w, y_att_ready)

                def flip_for_qkv(t, b, half, last_f):
                    if ffn:
                        pe.wait_ge(ln_f_ready, t + 1)
                        pe.wait_ge(flip_f_copied, last_f)
                        turn(ln_f[half], flip_q_ready)
                    else:
                        pe.wait_ge(ln_a_ready, t + 1)
                        wait(pe, flip_q_copied, t)
                        turn(normed[half], flip_q_ready)

                def ffn_product(t, b, half):
                    pe.wait_ge(flip_f_copied, t + 1)
                    wait(pe, x2_ready, t)
                    rows_times(y_ffn, flip_f, w["ffn"], y_ffn_ready)

                def bank_free(t, use):
                    if use >= 2:
                        tt, before = t, use - 2
                    else:
                        tt, before = t - 1, USES + use - 2
                    if before >= NC:
                        wait(pe, v_copied, V_USES * tt + before - NC + 1)
                    elif qkv == "b":
                        wait(pe, swap_ready, NC * tt + before + 1)
                        wait(pe, cos_ready, NC * tt + before + 1)
                    else:
                        wait(pe, rest_ready, NC * tt + before + 1)

                def projections(t, b, half):
                    pe.wait_ge(flip_q_copied, t + 1)
                    for c, (kind, at_c) in enumerate(chunks):
                        bank_free(t, c)
                        rows = P if kind == "q" else KW
                        lhs = (W_Q if kind == "q" else W_K)[:, :, at_c * P:at_c * P + rows]
                        for e in range(EC):
                            mm = nc.tensor.matmul(proj[c % 2][0:rows, :], lhs[:, e, :], flip_q[:, e, :],
                                                  start=(e == 0), stop=(e == EC - 1))
                        mm.then_inc(proj_ready, 1)
                    per = SUB // V_USES
                    for use in range(V_USES):
                        bank_free(t, NC + use)
                        bank = proj[(NC + use) % 2]
                        for k in range(per):
                            s = use * per + k
                            for e in range(EC):
                                mm = nc.tensor.matmul(bank[:, k * VW:(k + 1) * VW], flip_q[:, e, s * P:(s + 1) * P],
                                                      W_V[:, e, :], start=(e == 0), stop=(e == EC - 1))
                        mm.then_inc(proj_ready, 1)

                def body(i, n, u):
                    if at("F", i, n, u):
                        flip_for_ffn(*at("F", i, n, u))
                    if ffn and at("A", i, n, u):
                        out_projection(*at("A", i, n, u))
                    if at("Q", i, n, u):
                        t = i - off["Q"]
                        flip_for_qkv(*at("Q", i, n, u), min(t + 2, TILES) if isinstance(i, int) else t + 2)
                    if at("F", i, n, u):
                        ffn_product(*at("F", i, n, u))
                    if at("Q", i, n, u):
                        projections(*at("Q", i, n, u))

                rounds(pe, body)

            @block.scalar
            def _(act):
                def copy_for_ffn(t, b, half):
                    act.wait_ge(flip_f_ready, t + 1)
                    wait(act, y_ffn_ready, t)
                    nc.scalar.copy(flip_f[:, :, :], flipped[:, :, :]).then_inc(flip_f_copied, 1)

                def copy_for_qkv(t, b, half):
                    act.wait_ge(flip_q_ready, t + 1)
                    wait(act, proj_ready, USES * t)
                    nc.scalar.copy(flip_q[:, :, :], flipped[:, :, :]).then_inc(flip_q_copied, 1)

                def high(t, c):
                    rows = P if chunks[c][0] == "q" else KW
                    wait(act, parts_stored[c], 16 * PARTS * t)
                    if qkv == "a":
                        act.wait_ge(proj_ready, USES * t + c + 1)
                        src = proj[c % 2]
                    else:
                        act.wait_ge(turned_ready, NC * t + c + 1)
                        src = turned[c]
                    nc.scalar.copy(part[c][0][0:rows, :], src[0:rows, :]).then_inc(high_ready, 1)

                def mid(t, c):
                    rows = P if chunks[c][0] == "q" else KW
                    act.wait_ge(rest_ready, NC * t + c + 1)
                    nc.scalar.copy(part[c][1][0:rows, :], rest[c][0:rows, :]).then_inc(mid_ready, 1)

                def values(t):
                    per = SUB // V_USES
                    wait(act, v_stored, 16 * NG * t)
                    for use in range(V_USES):
                        act.wait_ge(proj_ready, USES * t + NC + use + 1)
                        src = proj[(NC + use) % 2][:, 0:per * VW].rearrange("p (s g v) -> p s g v", s=per, g=NG)
                        for s in range(per):
                            ins = nc.scalar.copy(v_tile[:, :, use * per + s, :], src[:, s, :, :])
                        ins.then_inc(v_copied, 1)

                def deviation(count):
                    act.wait_ge(ln_step, (2 * SUB + 1) * count + 2 * SUB)
                    nc.scalar.activation(std[:, :], moments[:, :, 1], ACT.Sqrt, bias=const["eps"][:, 0:1])\
                        .then_inc(std_ready, 1)

                def body(i, n, u):
                    if at("F", i, n, u):
                        copy_for_ffn(*at("F", i, n, u))
                    if at("Q", i, n, u):
                        copy_for_qkv(*at("Q", i, n, u))
                    if at("A", i, n, u):
                        deviation(norms_before("A", at("A", i, n, u)[0]))
                    if qkv and at("F", i, n, u):
                        deviation(norms_before("F", at("F", i, n, u)[0]))
                    if at("Q", i, n, u):
                        t = at("Q", i, n, u)[0]
                        if qkv == "b":
                            values(t)
                        for c in range(NC):
                            high(t, c)
                            if c:
                                mid(t, c - 1)
                        mid(t, NC - 1)
                        if qkv == "a":
                            values(t)

                rounds(act, body)

            @block.gpsimd
            def _(pool):
                def add_bias(t, b, half):
                    pool.wait_ge(x1_ready, t + 1)
                    wait(pool, x2_ready, t - 1)
                    nc.gpsimd.tensor_tensor(x1_bias[half][:, :, :], x1[half][:, :, :], w["bias"][:, :, :], ALU.add)\
                        .then_inc(x1_bias_ready, 1)

                def turn_pairs(t, c, half):
                    kind, at_c = chunks[c]
                    rows = P if kind == "q" else KW
                    pool.wait_ge(swap_ready, NC * t + c + 1)
                    nc.gpsimd.tensor_tensor(swapped[c][0:rows, :], swapped[c][0:rows, :],
                                            sin[kind][:, at_c, half * BANK:(half + 1) * BANK], ALU.mult)\
                        .then_inc(turn_step, 1)
                    pool.wait_ge(turn_step, NC * t + c + 1)
                    pool.wait_ge(cos_ready, NC * t + c + 1)
                    nc.gpsimd.tensor_tensor(turned[c][0:rows, :], turned[c][0:rows, :], swapped[c][0:rows, :], ALU.add)\
                        .then_inc(turned_ready, 1)

                def low(t, c):
                    rows = P if chunks[c][0] == "q" else KW
                    pool.wait_ge(mid_ready, NC * t + c + 1)
                    nc.gpsimd.tensor_tensor(part[c][2][0:rows, :], rest[c][0:rows, :], part[c][1][0:rows, :],
                                            ALU.subtract).then_inc(low_ready, 1)

                def body(i, n, u):
                    if ffn and at("A", i, n, u):
                        add_bias(*at("A", i, n, u))
                    if at("Q", i, n, u):
                        t, b, half = at("Q", i, n, u)
                        if qkv == "b":
                            for c in range(NC):
                                turn_pairs(t, c, half)
                                if c:
                                    low(t, c - 1)
                            low(t, NC - 1)
                        else:
                            for c in range(NC):
                                low(t, c)

                if qkv == "b":
                    pool.wait_ge(tables_loaded, 64)
                rounds(pool, body)

            @block.vector
            def _(dve):
                def layer_norm(dst, src, count, ready):
                    for s in range(SUB):
                        nc.vector.bn_stats(stats[:, s, :], src[:, s, :]).then_inc(ln_step, 1)
                    for s in range(SUB):
                        dve.wait_ge(ln_step, (2 * SUB + 1) * count + s + 1)
                        apart(dve, const["spare"])
                        nc.vector.bn_aggr(moments[:, s, :], stats[:, s, :]).then_inc(ln_step, 1)
                    dve.wait_ge(std_ready, count + 1)
                    nc.vector.reciprocal(rstd[:, :], std[:, :]).then_inc(ln_step, 1)
                    dve.wait_ge(ln_step, (2 * SUB + 1) * (count + 1))
                    for s in range(SUB):
                        ins = nc.vector.tensor_scalar(dst[:, s, :], src[:, s, :], moments[:, s, 0:1], rstd[:, s:s + 1],
                                                      ALU.subtract, ALU.mult)
                    ins.then_inc(ready, 1)

                def reciprocals(t, b, half):
                    dve.wait_ge(sums_loaded[half], (b + 1) * 16)
                    wait(dve, recip_stored[half], b * 16)
                    nc.vector.reciprocal(recip[half][:, :], sums[half][:, :]).then_inc(recip_ready, 1)

                def normalise(t, b, half):
                    dve.wait_ge(att_loaded[half], (b + 1) * 16 * 2 * EC)
                    nc.vector.tensor_tensor(att[half][:, :, :], att[half][:, :, :], recip_wide[half][:, :, :], ALU.mult)\
                        .then_inc(att_ready, 1)

                def first_residual(t, b, half, count):
                    dve.wait_ge(x_loaded[half], (b + 1) * 16)
                    if ffn:
                        dve.wait_ge(y_att_ready, t + 1)
                        wait(dve, x1_bias_ready, t - 1)
                        nc.vector.tensor_tensor(x1[half][:, :, :], y_att[:, :, :], x_tile[half][:, :, :], ALU.add)\
                            .then_inc(x1_ready, 1)
                        dve.wait_ge(x1_ready, t + 1)
                        wait(dve, flip_f_ready, t - 1)
                        layer_norm(normed[half], x1[half], count, ln_a_ready)
                    else:
                        wait(dve, flip_q_ready, t - 1)
                        layer_norm(normed[half], x_tile[half], count, ln_a_ready)

                def second_residual(t, b, half, count):
                    dve.wait_ge(y_ffn_ready, t + 1)
                    dve.wait_ge(x1_bias_ready, t + 1)
                    wait(dve, x2_stored[half], b * 16)
                    nc.vector.tensor_tensor(x2[half][:, :, :], y_ffn[:, :, :], x1_bias[half][:, :, :], ALU.add)\
                        .then_inc(x2_ready, 1)
                    if qkv:
                        dve.wait_ge(x2_ready, t + 1)
                        wait(dve, flip_q_ready, t - 1)
                        layer_norm(ln_f[half], x2[half], count, ln_f_ready)

                def leave(t, c):
                    rows = P if chunks[c][0] == "q" else KW
                    dve.wait_ge(high_ready, NC * t + c + 1)
                    wait(dve, low_ready, NC * (t - 1) + c + 1)
                    src = proj[c % 2] if qkv == "a" else turned[c]
                    nc.vector.tensor_tensor(rest[c][0:rows, :], src[0:rows, :], part[c][0][0:rows, :], ALU.subtract)\
                        .then_inc(rest_ready, 1)

                def swap_pairs(t, c, half):
                    kind, at_c = chunks[c]
                    rows = P if kind == "q" else KW
                    dve.wait_ge(proj_ready, USES * t + c + 1)
                    wait(dve, rest_ready, NC * (t - 1) + c + 1)
                    wait(dve, turned_ready, NC * (t - 1) + c + 1)
                    apart(dve, const["spare"])
                    nc.vector.stream_shuffle(swapped[c][0:rows, :], proj[c % 2][0:rows, :], [r ^ 1 for r in range(32)])\
                        .then_inc(swap_ready, 1)
                    nc.vector.tensor_tensor(turned[c][0:rows, :], proj[c % 2][0:rows, :],
                                            cos[kind][:, at_c, half * BANK:(half + 1) * BANK], ALU.mult)\
                        .then_inc(cos_ready, 1)

                def body(i, n, u):
                    if at("R", i, n, u):
                        reciprocals(*at("R", i, n, u))
                    if ffn and at("O", i, n, u):
                        normalise(*at("O", i, n, u))
                    if at("A", i, n, u):
                        first_residual(*at("A", i, n, u), norms_before("A", at("A", i, n, u)[0]))
                    if at("F", i, n, u):
                        second_residual(*at("F", i, n, u), norms_before("F", at("F", i, n, u)[0]))
                    if at("Q", i, n, u):
                        t, b, half = at("Q", i, n, u)
                        if qkv == "b":
                            swap_pairs(t, 0, half)
                            swap_pairs(t, 1, half)
                            leave(t, 0)
                            swap_pairs(t, 2, half)
                            leave(t, 1)
                            leave(t, 2)
                        else:
                            for c in range(NC):
                                leave(t, c)

                if qkv == "b":
                    dve.wait_ge(tables_loaded, 64)
                rounds(dve, body)


def attention_phase(nc, tag, const, q_scr, k_scr, v_scr, out_scr, causal, shared_kv, scale):
    KH = 1 if shared_kv else G
    KROWS = NG * KH * D
    LOADS = 2 * len(Q_PARTS)
    ST = SM = 3

    def seen_by(i):
        return (P * i if causal else 0), T

    def cuts(lo, hi, width):
        return [(max(lo, k), min(hi, k + width)) for k in range(0, T, width) if max(lo, k) < min(hi, k + width)]

    UNITS = [(j, i, lo, hi) for j in range(G) for i in range(NT)
             for lo, hi in cuts(0, P * (i + 1) if causal else T, BANK)]
    U = len(UNITS)
    TURNS = [(i, j, lo, hi) for i in range(NT) for j in range(G) for lo, hi in cuts(*seen_by(i), BANK)]
    S = len(TURNS)
    PIECES = [cuts(*seen_by(i), BANK // 2) for i in range(NT)]
    FIRST_TURN = [next(n for n, t in enumerate(TURNS) if t[0] == i) for i in range(NT)] + [S]
    FIRST_PIECE = [sum(len(p) for p in PIECES[:i]) for i in range(NT + 1)]
    V = FIRST_PIECE[NT]
    HEAD_START = U // 4

    def turn_of(i, j, hi):
        return max(n for n, t in enumerate(TURNS) if t[:2] == (i, j) and t[2] < hi) + 1

    def use_free(banks, n):
        return banks if n == 0 else 1

    def spread():
        cost = []
        for n, (i, j, lo, hi) in enumerate(TURNS):
            ends = n + 1 == S or TURNS[n + 1][:2] != (i, j)
            piece = PIECES[i - 1][j] if ends and i and j < len(PIECES[i - 1]) else (0, 0)
            cost.append(hi - lo + 2.2 * (piece[1] - piece[0]))
        whole = sum(cost) + 2.2 * sum(hi - lo for lo, hi in PIECES[-1])
        return [round(U * sum(cost[:n + 1]) / whole) for n in range(S)]

    QUOTA = spread()

    with ExitStack() as ctx:
        sb = lambda name, shape, dt=F32: ctx.enter_context(nc.sbuf_tensor(tag + name, shape, dt))
        ps = lambda name, shape: ctx.enter_context(nc.psum_tensor(tag + name, shape, F32))
        sem = lambda name: ctx.enter_context(nc.semaphore(tag + name))

        q_ops = [sb(f"q_ops{g}", [ROWS, G, T], BF16) for g in range(NG)]
        k_ops = [sb(f"k_ops{g}", [ROWS, KH, T], BF16) for g in range(NG)]
        v_in = [sb(f"v_in{g}", [P, NT, KH, D]) for g in range(NG)]
        v_ones = [sb(f"v_ones{g}", [P, NT, KH, 2 * D]) for g in range(NG)]
        probs = [sb(f"probs{k}", [P, G, T]) for k in range(2)]
        out_tile = [sb(f"out_tile{k}", [P, T]) for k in range(2)]
        bank_max = sb("bank_max", [P, 2, G, NT])
        row_max = sb("row_max", [P, G, NT])
        max_parts = sb("max_parts", [P, 2, G * NT], BF16)
        max_turned = [sb(f"max_turned{k}", [P, 2, G * NT], BF16) for k in range(2)]
        scores_t = [ps(f"scores_t{k}", [P, BANK]) for k in range(ST)]
        out_acc = ps("out_acc", [P, T])
        scores = [ps(f"scores{k}", [P, BANK]) for k in range(SM)]

        qk_loaded = [sem(f"qk_loaded{g}") for g in range(NG)]
        v_loaded = [sem(f"v_loaded{g}") for g in range(NG)]
        max_loaded = [sem(f"max_loaded{g}") for g in range(NG)]
        const_ready = sem("const_ready")
        v_ready = sem("v_ready")
        scores_ready, scores_free = sem("scores_ready"), sem("scores_free")
        max_step, max_ready = sem("max_step"), sem("max_ready")
        scores_t_ready, probs_ready, probs_free = sem("scores_t_ready"), sem("probs_ready"), sem("probs_free")
        out_copied = sem("out_copied")
        out_stored = [sem(f"out_stored{k}") for k in range(2)]

        with nc.Block() as block:
            @block.sync
            def _(sp):
                def load(b, g):
                    for k in range(len(Q_PARTS)):
                        src = q_scr[bass.ds((b * PARTS + Q_PARTS[k]) * E + g * G * D, G * D), :]
                        sp.dma_start(q_ops[g][D * k:D * (k + 1), :, :], src.rearrange("(j d) t -> d j t", d=D))\
                            .then_inc(qk_loaded[g], 16)
                        src = k_scr[bass.ds((b * PARTS + K_PARTS[k]) * KROWS + g * KH * D, KH * D), :]
                        sp.dma_start(k_ops[g][D * k:D * (k + 1), :, :], src.rearrange("(j d) t -> d j t", d=D))\
                            .then_inc(qk_loaded[g], 16)

                def load_v(b, g):
                    sp.dma_start(v_in[g][:, :, :, :].rearrange("p i j d -> p (i j d)"),
                                 v_scr[bass.ds((b * NG + g) * P, P), 0:NT * KH * D]).then_inc(v_loaded[g], 16)

                def place_max(b, g):
                    group = b * NG + g
                    sp.wait_ge(max_ready, group + 1)
                    apart(sp, const["spare"])
                    for k in range(2):
                        for a in range(4):
                            dst = q_ops[g][SPLIT + k:SPLIT + k + 1, :, :].rearrange(
                                "o j (i a r) -> o (j i) a r", a=4, r=32)[:, :, a, :]
                            sp.dma_start(dst, max_turned[g % 2][32 * a:32 * a + 32, k, :]).then_inc(max_loaded[g], 16)

                def store(b, g):
                    group = b * NG + g
                    sp.wait_ge(out_copied, group + 2)
                    apart(sp, const["spare"])
                    sp.dma_start(out_scr[bass.ds(group * P, P), :], out_tile[g % 2][:, :]).then_inc(out_stored[g % 2], 16)

                def batch_row(b, last):
                    for g in range(NG):
                        if g + 1 < NG:
                            place_max(b, g + 1)
                        elif not last:
                            place_max(b + 1, 0)
                        if not last:
                            sp.wait_ge(scores_t_ready, S * (b * NG + g + 1))
                            apart(sp, const["spare"])
                            load(b + 1, g)
                            sp.wait_ge(v_ready, b * NG + g + 1)
                            apart(sp, const["spare"])
                            load_v(b + 1, g)
                        store(b, g)

                for k in range(2):
                    sp.sem_inc(out_stored[k], 16)
                for g in range(NG):
                    load(0, g)
                    load_v(0, g)
                place_max(0, 0)
                with sp.Fori(0, BATCH - 1) as b:
                    batch_row(b, False)
                batch_row(BATCH - 1, True)
                for k in range(2):
                    sp.wait_ge(out_stored[k], 16 + 16 * (BATCH * NG // 2))

            @block.gpsimd
            def _(pool):
                for g in range(NG):
                    nc.gpsimd.memset(k_ops[g][SPLIT:ROWS, :, :], -1.0).then_inc(const_ready, 1)
                for g in range(NG):
                    pool.wait_ge(const_ready, NG)
                    nc.gpsimd.memset(v_ones[g][:, :, :, D:2 * D], 1.0).then_inc(const_ready, 1)

                def batch_row(b, first):
                    for g in range(NG):
                        pool.wait_ge(v_loaded[g], 16 * (b + 1))
                        if not first:
                            pool.wait_ge(probs_free, V * ((b - 1) * NG + g + 2))
                        apart(pool, const["spare"])
                        nc.gpsimd.tensor_copy(v_ones[g][:, :, :, 0:D], v_in[g][:, :, :, :]).then_inc(v_ready, 1)

                batch_row(0, True)
                with pool.Fori(1, BATCH) as b:
                    batch_row(b, False)

            @block.tensor
            def _(pe):
                pe.sem_inc(probs_free, V)
                pe.wait_ge(const_ready, 2 * NG)

                def max_unit(b, g, n):
                    j, i, lo, hi = UNITS[n]
                    if n == 0:
                        pe.wait_ge(qk_loaded[g], 16 * LOADS * (b + 1))
                    pe.wait_ge(scores_free, U * (b * NG + g) + n + use_free(SM, g * U + n))
                    bank = scores[(g * U + n) % SM]
                    hides = causal and hi == P * (i + 1)
                    mm = nc.tensor.matmul(bank[:, 0:hi - lo], q_ops[g][0:SPLIT, j, P * i:P * (i + 1)],
                                          k_ops[g][0:SPLIT, j % KH, lo:hi], start=True, stop=True)
                    if hides:
                        mm = nc.tensor.matmul(bank[:, hi - P - lo:hi - lo], const["ident16"][:, :],
                                              const["hide_qk"][:, :], start=False, stop=True, skip_group_check=True)
                    mm.then_inc(scores_ready, 1)

                def transposed_scores(b, g, n):
                    i, j, lo, hi = TURNS[n]
                    pe.wait_ge(probs_ready, S * (b * NG + g) + n + use_free(ST, g * S + n))
                    bank = scores_t[(g * S + n) % ST]
                    hides = causal and lo == P * i
                    mm = nc.tensor.matmul(bank[:, 0:hi - lo], k_ops[g][:, j % KH, P * i:P * (i + 1)],
                                          q_ops[g][:, j, lo:hi], start=True, stop=True)
                    if hides:
                        mm = nc.tensor.matmul(bank[:, 0:P], const["ident16"][:, :], const["hide_kq"][:, :],
                                              start=False, stop=True, skip_group_check=True)
                    mm.then_inc(scores_t_ready, 1)

                def weigh_values(b, g, i, k):
                    group = b * NG + g
                    lo, hi = PIECES[i][k]
                    if i == 0 and k == 0:
                        pe.wait_ge(v_ready, group + 1)
                        pe.wait_ge(out_copied, group + 1)
                    pe.wait_ge(probs_ready, S * group + turn_of(i, G - 1, hi) + ST)
                    for j in range(G):
                        mm = nc.tensor.matmul(out_acc[32 * j:32 * j + 32, lo:hi], v_ones[g][:, i, j % KH, :],
                                              probs[i % 2][:, j, lo:hi], start=(i == 0 and lo % BANK == 0), stop=True,
                                              skip_group_check=True)
                    mm.then_inc(probs_free, 1)

                def window(b, g, last):
                    pe.wait_ge(max_loaded[g], 16 * 8 * (b + 1))
                    units = []
                    for ahead, ns in ((1, range(HEAD_START, U)), (2, range(HEAD_START))):
                        if not (last and g + ahead >= NG):
                            units += [(b + (g + ahead) // NG, (g + ahead) % NG, n) for n in ns]
                    taken = 0
                    for n, (i, j, lo, hi) in enumerate(TURNS):
                        transposed_scores(b, g, n)
                        while taken < min(QUOTA[n], len(units)):
                            max_unit(*units[taken])
                            taken += 1
                        if hi == T and i and j < len(PIECES[i - 1]):
                            weigh_values(b, g, i - 1, j)
                    for k in range(len(PIECES[-1])):
                        for m in range((len(units) - taken) // (len(PIECES[-1]) - k)):
                            max_unit(*units[taken])
                            taken += 1
                        weigh_values(b, g, NT - 1, k)

                for n in range(U):
                    max_unit(0, 0, n)
                for n in range(HEAD_START):
                    max_unit(0, 1, n)
                nc.disable_value_cache = True
                with pe.Fori(0, BATCH - 1) as b:
                    for g in range(NG):
                        window(b, g, False)
                nc.disable_value_cache = False
                for g in range(NG):
                    window(BATCH - 1, g, True)

            @block.scalar
            def _(act):
                act.sem_inc(probs_ready, ST)
                act.sem_inc(out_copied, 1)

                with act.Fori(0, BATCH) as b:
                    for g in range(NG):
                        group = b * NG + g
                        for n, (i, j, lo, hi) in enumerate(TURNS):
                            if j == 0:
                                before = (i - 2) % NT
                                used = FIRST_PIECE[before] + sum(p[0] < hi for p in PIECES[before])
                                if used > FIRST_PIECE[before]:
                                    act.wait_ge(probs_free, V * (group + (i >= 2)) + used)
                            act.wait_ge(scores_t_ready, S * group + n + 1)
                            nc.scalar.activation(probs[i % 2][:, j, lo:hi], scores_t[(g * S + n) % ST][:, 0:hi - lo],
                                                 ACT.Exp, scale=scale).then_inc(probs_ready, 1)
                        act.wait_ge(probs_free, V * (group + 2))
                        act.wait_ge(out_stored[g % 2], 16 * (b * NG // 2 + g // 2 + 1))
                        nc.scalar.copy(out_tile[g % 2][:, :], out_acc[:, :]).then_inc(out_copied, 1)

            @block.vector
            def _(dve):
                dve.sem_inc(scores_free, SM)

                def maxima(b, g):
                    group = b * NG + g
                    for n, (j, i, lo, hi) in enumerate(UNITS):
                        dve.wait_ge(scores_ready, U * group + n + 1)
                        alone = causal and i < BANK // P
                        dst = row_max[:, j, i:i + 1] if alone else bank_max[:, lo // BANK, j, i:i + 1]
                        nc.vector.tensor_reduce(dst, scores[(g * U + n) % SM][:, 0:hi - lo], AX.X, ALU.max)\
                            .then_inc(scores_free, 1)
                    dve.wait_ge(scores_free, U * (group + 1) + SM)
                    i0 = BANK // P if causal else 0
                    nc.vector.tensor_tensor(row_max[:, :, i0:NT], bank_max[:, 0, :, i0:NT], bank_max[:, 1, :, i0:NT],
                                            ALU.max).then_inc(max_step, 1)
                    dve.wait_ge(max_step, 3 * group + 1)
                    nc.vector.tensor_copy(max_parts[:, 0, :], row_max[:, :, :].rearrange("p j i -> p (j i)"))\
                        .then_inc(max_step, 1)
                    dve.wait_ge(max_step, 3 * group + 2)
                    nc.vector.tensor_tensor(max_parts[:, 1, :], row_max[:, :, :].rearrange("p j i -> p (j i)"),
                                            max_parts[:, 0, :], ALU.subtract).then_inc(max_step, 1)
                    dve.wait_ge(max_step, 3 * group + 3)
                    nc.vector.transpose(max_turned[g % 2][:, :, :].rearrange("p k c -> p (k c)"),
                                        max_parts[:, :, :].rearrange("p k c -> p (k c)")).then_inc(max_ready, 1)

                with dve.Fori(0, BATCH) as b:
                    for g in range(NG):
                        maxima(b, g)


def build(nc, x, qkvT, outT, q_b, k_b, v_b, out_b, ffn, bias, lora_aT, lora_b, cos_q, sin_q, cos_k, sin_k, out):
    scr = lambda name, shape, dt=F32: nc.dram_tensor(name, shape, dt, kind="Internal").ap()
    x_rows = x.rearrange("b t e -> (b t) e")
    out_rows = out.rearrange("b t e -> (b t) e")
    q_scr = [scr(f"q_parts_{l}", [BATCH * PARTS * E, T], BF16) for l in "ab"]
    k_scr = [scr("k_parts_a", [BATCH * PARTS * E, T], BF16), scr("k_parts_b", [BATCH * PARTS * E // G, T], BF16)]
    v_scr = [scr("v_a", [BATCH * NG * P, NT * G * D]), scr("v_b", [BATCH * NG * P, NT * D])]
    att_scr = [scr(f"attended_{l}", [BATCH * NG * P, T]) for l in "ab"]
    recip_scr = [scr(f"recip_{l}", [BATCH * H, T]) for l in "ab"]
    x_mid = scr("x_mid", [BATCH * T, E])

    with ExitStack() as ctx:
        sb = lambda name, shape, dt=F32: ctx.enter_context(nc.sbuf_tensor(name, shape, dt))
        w = {"qkvT": sb("w_qkvT", [P, EC, 3 * E]), "outT": sb("w_outT", [P, EC, E]), "q_b": sb("w_q_b", [P, EC, E]),
             "k_b": sb("w_k_b", [P, EC, E // G]), "v_b": sb("w_v_b", [P, EC, E // G]), "out_b": sb("w_out_b", [P, EC, E]),
             "ffn": sb("w_ffn", [P, EC, E]), "bias": sb("w_bias", [P, SUB, E])}
        const = {"spare": ctx.enter_context(nc.semaphore("spare")), "eps": sb("eps", [P, 1]), "ident": sb("ident", [P, P]), "ident16": sb("ident16", [P, P], BF16),
                 "hide_qk": sb("hide_qk", [P, P], BF16), "hide_kq": sb("hide_kq", [P, P], BF16)}
        src = {"qkvT": qkvT, "outT": outT, "q_b": q_b, "k_b": k_b, "v_b": v_b, "out_b": out_b, "ffn": ffn,
               "bias": bias, "lora_aT": lora_aT, "lora_b": lora_b}
        tables = {"cos_q": cos_q, "sin_q": sin_q, "cos_k": cos_k, "sin_k": sin_k}
        weights_phase(nc, src, w, const)
        token_phase(nc, "t1_", w, const, x_rows, None, None, None, None, "a", q_scr[0], k_scr[0], v_scr[0], None)
        attention_phase(nc, "a_", const, q_scr[0], k_scr[0], v_scr[0], att_scr[0], causal=True, shared_kv=False,
                        scale=float(D) ** -0.5)
        token_phase(nc, "t2_", w, const, x_rows, x_mid, att_scr[0], recip_scr[0], w["outT"], "b",
                    q_scr[1], k_scr[1], v_scr[1], tables)
        attention_phase(nc, "b_", const, q_scr[1], k_scr[1], v_scr[1], att_scr[1], causal=False, shared_kv=True,
                        scale=float(E) ** -0.5)
        token_phase(nc, "t3_", w, const, x_mid, out_rows, att_scr[1], recip_scr[1], w["out_b"], None,
                    None, None, None, None)


def rope_tables():
    f = np.float32
    inv = (f(1.0) / (f(10000.0) ** (np.arange(0, E, 2, dtype=f) / f(E)))).astype(f)
    ang = (np.arange(T, dtype=f)[None, :] * inv[:, None]).astype(f)
    cos, sin = np.cos(ang).astype(f), np.sin(ang).astype(f)
    wide = lambda a: np.repeat(a, 2, axis=0)
    signs = lambda a: np.stack([-a, a], axis=1).reshape(-1, a.shape[1])
    heads = lambda a: np.concatenate([a] * NG, axis=0)
    half = D // 2
    return {"cos_q": wide(cos), "sin_q": signs(sin), "cos_k": heads(wide(cos[:half])), "sin_k": heads(signs(sin[:half]))}


def kernel(**inputs):
    import concourse.bacc as bacc
    from concourse.bass_utils import run_bass_kernel_spmd

    a = {k: np.asarray(v) for k, v in inputs.items()}
    arrays = {
        "x": a["L0_attn_a_x"], "qkvT": a["L0_attn_a_W_qkv"].T, "outT": a["L0_attn_a_W_out"].T,
        "q_b": a["L0_attn_b_Wq"], "k_b": a["L0_attn_b_Wk"], "v_b": a["L0_attn_b_Wv"], "out_b": a["L0_attn_b_Wo"],
        "ffn": a["L0_ffn_kernel"], "bias": a["L0_ffn_bias"], "lora_aT": a["L0_ffn_a"].T, "lora_b": a["L0_ffn_b"],
        **rope_tables(),
    }
    nc = bacc.Bacc("TRN2", target_bir_lowering=False, num_devices=1)
    maps, args = {}, []
    for name, value in arrays.items():
        value = np.ascontiguousarray(value)
        maps[f"in_{name}"] = value
        args.append(nc.dram_tensor(f"in_{name}", value.shape, mybir.dt.from_np(value.dtype), kind="ExternalInput").ap())
    out = nc.dram_tensor("out_x", (BATCH, T, E), F32, kind="ExternalOutput").ap()
    build(nc, *args, out)
    result = run_bass_kernel_spmd(nc, [maps], core_ids=[0])
    return result.results[0]["out_x"]
```

```python
from contextlib import ExitStack

import numpy as np
import concourse.bass as bass
from concourse import mybir

F32 = mybir.dt.float32
BF16 = mybir.dt.bfloat16
ALU = mybir.AluOpType
ACT = mybir.ActivationFunctionType
AX = mybir.AxisListType

P = 128
BATCH, T, E = 16, 1024, 256
H, D = 16, 16
G = 4
NG = H // G
NT = T // P
BANK = 512
EC = E // P
SUB = BANK // P
TILES = BATCH * T // BANK
PARTS = 3
SPLIT = 6 * D
ROWS = SPLIT + 2
Q_PARTS = (0, 0, 0, 1, 1, 2)
K_PARTS = (0, 1, 2, 0, 1, 0)
HIDDEN = -1.0e30
EPS = 1e-5
QMAX = 7.0
ROUND = 12582912.0
LORA = 16


def wait(eng, sem, value):
    if not isinstance(value, int) or value > 0:
        eng.wait_ge(sem, value)


def apart(eng, spare):
    eng.sem_inc(spare, 1)


def weights_phase(nc, src, w, const):
    with ExitStack() as ctx:
        sb = lambda name, shape, dt=F32: ctx.enter_context(nc.sbuf_tensor(name, shape, dt))
        sem = lambda name: ctx.enter_context(nc.semaphore(name))
        ffn_raw = sb("ffn_raw", [P, EC, E])
        lora_aT = sb("lora_aT", [LORA, E])
        lora_b = sb("lora_b", [LORA, E])
        abs_max = sb("abs_max", [P, 1])
        all_max = sb("all_max", [P, 1])
        scale = sb("scale", [P, 1])
        per_scale = sb("per_scale", [P, 1])
        quant = sb("quant", [P, EC, E])
        lora = ctx.enter_context(nc.psum_tensor("lora", [P, EC, E], F32))
        loaded, ffn_loaded, lora_loaded = sem("weights_loaded"), sem("ffn_loaded"), sem("lora_loaded")
        zeroed, built, rowmax, allmax = sem("zeroed"), sem("masks_built"), sem("row_max"), sem("core_max")
        step, lora_done = sem("quant_step"), sem("lora_done")

        with nc.Block() as block:
            @block.sync
            def _(sp):
                sp.dma_start(ffn_raw[:, :, :], src["ffn"].rearrange("(c p) n -> p c n", p=P)).then_inc(ffn_loaded, 16)
                sp.dma_start(lora_aT[:, :], src["lora_aT"]).then_inc(lora_loaded, 16)
                sp.dma_start(lora_b[:, :], src["lora_b"]).then_inc(lora_loaded, 16)
                count = 0
                for name in ("qkvT", "outT", "q_b", "k_b", "v_b", "out_b"):
                    sp.dma_start(w[name][:, :, :], src[name].rearrange("(c p) n -> p c n", p=P)).then_inc(loaded, 16)
                    count += 16
                bias = src["bias"].rearrange("(a n) -> a n", a=1)
                sp.dma_start(w["bias"][:, 0, :], bias.broadcast_to([P, E])).then_inc(loaded, 16)
                for s in range(1, SUB):
                    sp.dma_start(w["bias"][:, s, :], bias.broadcast_to([P, E])).then_inc(loaded, 16)
                count += 16 * SUB
                sp.wait_ge(loaded, count)

            @block.gpsimd
            def _(pool):
                nc.gpsimd.memset(const["eps"][:, :], EPS).then_inc(built, 1)
                for m in ("ident", "hide"):
                    nc.gpsimd.memset(const[m][:, :], 0.0).then_inc(zeroed, 1)
                pool.wait_ge(zeroed, 2)
                nc.gpsimd.affine_select(out=const["ident"][:, :], in_=const["ident"][:, :], compare_op=ALU.not_equal,
                                        fill=1.0, base=0, pattern=[[-1, P]], channel_multiplier=1).then_inc(built, 1)
                nc.gpsimd.affine_select(out=const["hide"][:, BANK - P:], in_=const["hide"][:, BANK - P:],
                                        compare_op=ALU.is_ge, fill=HIDDEN, base=0, pattern=[[-1, P]],
                                        channel_multiplier=1).then_inc(built, 1)
                pool.wait_ge(built, 3)
                pool.wait_ge(rowmax, 1)
                nc.gpsimd.partition_all_reduce(all_max[:, :], abs_max[:, :], P,
                                               bass.bass_isa.ReduceOp.max).then_inc(allmax, 1)

            @block.tensor
            def _(pe):
                pe.wait_ge(lora_loaded, 32)
                for c in range(EC):
                    mm = nc.tensor.matmul(lora[:, c, :], lora_aT[:, c * P:(c + 1) * P], lora_b[:, :],
                                          start=True, stop=True)
                mm.then_inc(lora_done, 1)

            @block.vector
            def _(dve):
                done = [0]

                def then(ins):
                    done[0] += 1
                    ins.then_inc(step, 1)
                    dve.wait_ge(step, done[0])

                dve.wait_ge(ffn_loaded, 16)
                nc.vector.tensor_reduce(abs_max[:, :], ffn_raw[:, :, :], AX.XY, ALU.max,
                                        apply_absolute_value=True).then_inc(rowmax, 1)
                dve.wait_ge(allmax, 1)
                then(nc.vector.tensor_scalar(scale[:, :], all_max[:, :], 1.0 / QMAX, None, ALU.mult))
                then(nc.vector.reciprocal(per_scale[:, :], scale[:, :]))
                then(nc.vector.tensor_scalar(quant[:, :, :], ffn_raw[:, :, :], per_scale[:, 0:1], ROUND,
                                             ALU.mult, ALU.add))
                then(nc.vector.tensor_scalar(quant[:, :, :], quant[:, :, :], ROUND, -8.0, ALU.subtract, ALU.max))
                then(nc.vector.tensor_scalar(quant[:, :, :], quant[:, :, :], QMAX, scale[:, 0:1], ALU.min, ALU.mult))
                dve.wait_ge(lora_done, 1)
                then(nc.vector.tensor_tensor(w["ffn"][:, :, :], lora[:, :, :], quant[:, :, :], ALU.add))


def token_phase(nc, tag, w, const, x_in, x_out, attended, recip_scr, out_w, qkv, q_scr, k_scr, v_scr, tables):
    ffn = attended is not None
    stages = {"a": ["O", "A", "T", "Q"], "b": ["R", "O", "A", "F", "Q", "S"], None: ["R", "O", "A", "T", "F"]}[qkv]
    off = {s: n for n, s in enumerate(stages)}
    chunks = {"a": [("q", 0), ("q", 1), ("k", 0), ("k", 1)], "b": [("q", 0), ("q", 1), ("k", 0)], None: []}[qkv]
    NC = len(chunks)
    SPLITS = "S" if qkv == "b" else "Q"
    TURN_F = "F" if qkv else "T"
    V_USES = 2 if qkv == "a" else 1
    USES = NC + V_USES
    BANKS = 2 if ffn else USES
    KW = {"a": P, "b": E // G, None: P}[qkv]
    VW = E if qkv == "a" else E // G
    VG = VW // NG
    W_Q, W_K, W_V = {"a": (w["qkvT"][:, :, 0:E], w["qkvT"][:, :, E:2 * E], w["qkvT"][:, :, 2 * E:3 * E]),
                     "b": (w["q_b"], w["k_b"], w["v_b"]), None: (None,) * 3}[qkv]

    with ExitStack() as ctx:
        sb = lambda name, shape, dt=F32: ctx.enter_context(nc.sbuf_tensor(tag + name, shape, dt))
        ps = lambda name, shape: ctx.enter_context(nc.psum_tensor(tag + name, shape, F32))
        sem = lambda name: ctx.enter_context(nc.semaphore(tag + name))
        two = lambda make, name, *a: [make(f"{name}{i}", *a) for i in range(2)]

        x_tile = two(sb, "x_tile", [P, SUB, E])
        normed = two(sb, "normed", [P, SUB, E])
        stats = sb("stats", [P, SUB, 6])
        moments = sb("moments", [P, SUB, 2])
        std = sb("std", [P, SUB])
        rstd = sb("rstd", [P, SUB])
        flipped = ps("flipped", [P, EC, BANK])
        if ffn:
            sums = two(sb, "sums", [P, BANK // 8])
            recip = two(sb, "recip", [P, BANK // 8])
            att = two(sb, "att", [P, EC, BANK])
            recip_wide = two(sb, "recip_wide", [P, EC, BANK])
            x1 = two(sb, "x1_", [P, SUB, E])
            x1_bias = two(sb, "x1_bias", [P, SUB, E])
            x2 = two(sb, "x2_", [P, SUB, E])
            ln_f = two(sb, "ln_f", [P, SUB, E])
            flip_f = sb("flip_f", [P, EC, BANK])
            y_att = ps("y_att", [P, SUB, E])
            y_ffn = [ps(f"y_ffn{k}", [P, SUB, E]) for k in range(1 if qkv else 2)]
        if qkv:
            flip_q = [sb(f"flip_q{k}", [P, EC, BANK]) for k in range(1 if ffn else 2)]
            part = [[sb(f"part{c}_{k}", [P, BANK], BF16) for k in range(PARTS)] for c in range(NC)]
            rest = [sb(f"rest{c}", [P, BANK]) for c in range(NC)]
            v_tile = sb("v_tile", [P, NG, SUB, VG])
            proj = [ps(f"proj{k}", [P, BANK]) for k in range(BANKS)]
        if qkv == "b":
            cos = {"q": sb("cos_q", [P, EC, T]), "k": sb("cos_k", [KW, 1, T])}
            sin = {"q": sb("sin_q", [P, EC, T]), "k": sb("sin_k", [KW, 1, T])}
            plain = [sb(f"plain{c}", [P, BANK]) for c in range(NC)]
            swapped = [sb(f"swapped{c}", [P, BANK]) for c in range(NC)]
            turned = [sb(f"turned{c}", [P, BANK]) for c in range(NC)]

        x_loaded, ln_a_ready = two(sem, "x_loaded"), sem("ln_a_ready")
        ln_step, std_ready = sem("ln_step"), sem("std_ready")
        if ffn:
            sums_loaded, recip_stored = two(sem, "sums_loaded"), two(sem, "recip_stored")
            recip_ready = sem("recip_ready")
            att_loaded, att_ready, y_att_ready = two(sem, "att_loaded"), sem("att_ready"), sem("y_att_ready")
            x1_ready, x1_bias_ready = sem("x1_ready"), sem("x1_bias_ready")
            flip_f_ready, flip_f_copied, y_ffn_ready = sem("flip_f_ready"), sem("flip_f_copied"), sem("y_ffn_ready")
            x2_ready, x2_stored = sem("x2_ready"), two(sem, "x2_stored")
        if ffn and qkv:
            ln_f_ready = sem("ln_f_ready")
        if qkv:
            flip_q_ready, flip_q_copied = sem("flip_q_ready"), sem("flip_q_copied")
            proj_ready, high_ready, rest_ready, mid_ready, low_ready = (sem(n) for n in (
                "proj_ready", "high_ready", "rest_ready", "mid_ready", "low_ready"))
            parts_stored = [sem(f"parts_stored{c}") for c in range(NC)]
            v_copied, v_stored = sem("v_copied"), sem("v_stored")
        if qkv == "b":
            plain_copied, swap_ready, cos_ready = sem("plain_copied"), sem("swap_ready"), sem("cos_ready")
            turn_step, turned_ready, tables_loaded = sem("turn_step"), sem("turned_ready"), sem("tables_loaded")

        def rounds(eng, body, ahead=0):
            first = 3
            for i in range(2 * first):
                body(i, i // 2, i % 2)
            with eng.Fori(first, TILES // 2 - ahead) as n:
                for u in range(2):
                    body(2 * n + u, n, u)
            for i in range(TILES - 2 * ahead, TILES + len(stages) - 1):
                body(i, i // 2, i % 2)

        def at(stage, i, n, u, ahead=0):
            if stage not in off:
                return None
            d = off[stage] - ahead
            t = i - d
            if isinstance(i, int) and not 0 <= t < TILES:
                return None
            return t, n + (u - d) // 2, (u - d) % 2

        def norms_before(stage, t):
            if not (qkv and ffn):
                return t
            if stage == "A":
                return t + (max(t - 1, 0) if isinstance(t, int) else t - 1)
            return t + (min(t + 2, TILES) if isinstance(t, int) else t + 2)

        def normalise(eng, t, b, half):
            eng.wait_ge(att_loaded[half], (b + 1) * 16 * 2 * EC)
            eng.tensor_tensor(att[half][:, :, :], att[half][:, :, :], recip_wide[half][:, :, :], ALU.mult)\
                .then_inc(att_ready, 1)

        with nc.Block() as block:
            @block.sync
            def _(sp):
                def load_sums(t, b, half):
                    wait(sp, recip_ready, t - 1)
                    apart(sp, const["spare"])
                    rows = attended[bass.ds(b * NG * P, NG * P), half * BANK:(half + 1) * BANK]
                    sp.dma_start(sums[half][:, :], rows.rearrange("(h r) (c t) -> h r c t", r=32, c=8)[:, D, :, :])\
                        .then_inc(sums_loaded[half], 16)

                def load_x(t, b, half):
                    wait(sp, x1_ready if ffn else ln_a_ready, t - 1)
                    apart(sp, const["spare"])
                    sp.dma_start(x_tile[half][:, :, :],
                                 x_in[bass.ds(b * T + half * BANK, BANK), :].rearrange("(s p) e -> p s e", p=P))\
                        .then_inc(x_loaded[half], 16)

                def store_recip(t, b, half):
                    sp.wait_ge(recip_ready, t + 1)
                    apart(sp, const["spare"])
                    sp.dma_start(recip_scr[bass.ds(b * H, H), half * BANK:(half + 1) * BANK]
                                 .rearrange("h (c t) -> h c t", c=8), recip[half][:, :])\
                        .then_inc(recip_stored[half], 16)

                def load_attended(t, b, half):
                    wait(sp, y_att_ready, t - 1)
                    apart(sp, const["spare"])
                    for c in range(EC):
                        src = attended[bass.ds((b * NG + 2 * c) * P, 2 * P), half * BANK:(half + 1) * BANK]
                        sp.dma_start(att[half][:, c, :], src.rearrange("(h r) t -> h r t", r=32)[:, 0:D, :])\
                            .then_inc(att_loaded[half], 16)

                def load_recip(t, b, half):
                    sp.wait_ge(recip_stored[half], (b + 1) * 16)
                    apart(sp, const["spare"])
                    for c in range(EC):
                        src = recip_scr[bass.ds(b * H + 8 * c, 8), half * BANK:(half + 1) * BANK]
                        sp.dma_start(recip_wide[half][:, c, :],
                                     src.rearrange("h (a t) -> h a t", a=1).broadcast_to([8, D, BANK]))\
                            .then_inc(att_loaded[half], 16)

                def store_x(t, b, half):
                    sp.wait_ge(x2_ready, t + 1)
                    apart(sp, const["spare"])
                    sp.dma_start(x_out[bass.ds(b * T + half * BANK, BANK), :].rearrange("(s p) e -> p s e", p=P),
                                 x2[half][:, :, :]).then_inc(x2_stored[half], 16)

                def store_parts(t, b, half):
                    for c, (kind, at_c) in enumerate(chunks):
                        rows = P if kind == "q" else KW
                        scr = q_scr if kind == "q" else k_scr
                        width = E if kind == "q" or qkv == "a" else KW
                        for k, (ready, count) in enumerate(((high_ready, NC * t + c + 1), (mid_ready, NC * t + c + 1),
                                                            (low_ready, NC * t + c + 1))):
                            sp.wait_ge(ready, count)
                            apart(sp, const["spare"])
                            sp.dma_start(scr[bass.ds((b * PARTS + k) * width + at_c * P, rows),
                                             half * BANK:(half + 1) * BANK], part[c][k][0:rows, :])\
                                .then_inc(parts_stored[c], 16)

                def store_v(t, b, half):
                    sp.wait_ge(v_copied, V_USES * (t + 1))
                    apart(sp, const["spare"])
                    for g in range(NG):
                        sp.dma_start(v_scr[bass.ds((b * NG + g) * P, P), half * SUB * VG:(half + 1) * SUB * VG],
                                     v_tile[:, g, :, :].rearrange("p s v -> p (s v)")).then_inc(v_stored, 16)

                def load_tables():
                    for name, dst in (("cos_q", cos["q"]), ("sin_q", sin["q"]),
                                      ("cos_k", cos["k"]), ("sin_k", sin["k"])):
                        sp.dma_start(dst[:, :, :], tables[name].rearrange("(c p) t -> p c t", p=dst.shape[0]))\
                            .then_inc(tables_loaded, 16)

                if ffn:
                    load_sums(0, 0, 0)
                else:
                    load_x(0, 0, 0)

                def body(i, n, u):
                    if at("R", i, n, u):
                        store_recip(*at("R", i, n, u))
                    if at("R", i, n, u, 1):
                        load_sums(*at("R", i, n, u, 1))
                    if at("R", i, n, u):
                        load_attended(*at("R", i, n, u))
                    if at("O", i, n, u, 0 if ffn else 1):
                        load_x(*at("O", i, n, u, 0 if ffn else 1))
                    if at("R", i, n, u):
                        load_recip(*at("R", i, n, u))
                    if qkv == "b" and isinstance(i, int) and i == off["Q"] - 2:
                        load_tables()
                    if at("F", i, n, u):
                        store_x(*at("F", i, n, u))
                    if at(SPLITS, i, n, u):
                        store_parts(*at(SPLITS, i, n, u))
                    if at("Q", i, n, u):
                        store_v(*at("Q", i, n, u))

                rounds(sp, body, 1)
                if ffn:
                    for half in range(2):
                        sp.wait_ge(x2_stored[half], 16 * BATCH)
                if qkv:
                    for c in range(NC):
                        sp.wait_ge(parts_stored[c], 16 * PARTS * TILES)
                    sp.wait_ge(v_stored, 16 * NG * TILES)
                    apart(sp, const["spare"])

            @block.tensor
            def _(pe):
                def turn(src, ready):
                    for c in range(EC):
                        for s in range(SUB):
                            mm = nc.tensor.transpose(flipped[:, c, s * P:(s + 1) * P],
                                                     src[:, s, c * P:(c + 1) * P], const["ident"][:, :])
                    mm.then_inc(ready, 1)

                def rows_times(dst, lhs, rhs, ready):
                    for s in range(SUB):
                        for c in range(EC):
                            mm = nc.tensor.matmul(dst[:, s, :], lhs[:, c, s * P:(s + 1) * P], rhs[:, c, :],
                                                  start=(c == 0), stop=(c == EC - 1))
                    mm.then_inc(ready, 1)

                def flip_for_ffn(t, b, half):
                    pe.wait_ge(ln_a_ready, t + 1)
                    if "Q" in off:
                        wait(pe, flip_q_copied, t - 1)
                    else:
                        wait(pe, flip_f_copied, t)
                    turn(normed[half], flip_f_ready)

                def out_projection(t, b, half):
                    pe.wait_ge(att_ready, t + 1)
                    wait(pe, x1_ready, t)
                    rows_times(y_att, att[half], out_w, y_att_ready)

                def flip_for_qkv(t, b, half, last_f=None):
                    if ffn:
                        pe.wait_ge(ln_f_ready, t + 1)
                        pe.wait_ge(flip_f_copied, last_f)
                        turn(ln_f[half], flip_q_ready)
                    else:
                        pe.wait_ge(ln_a_ready, t + 1)
                        wait(pe, flip_q_copied, t)
                        turn(normed[half], flip_q_ready)

                def ffn_product(t, b, half):
                    pe.wait_ge(flip_f_copied, t + 1)
                    wait(pe, x2_ready, t + 1 - len(y_ffn))
                    rows_times(y_ffn[half % len(y_ffn)], flip_f, w["ffn"], y_ffn_ready)

                def bank_free(t, use):
                    tt, before = (t, use - BANKS) if use >= BANKS else (t - 1, USES + use - BANKS)
                    if before >= NC:
                        wait(pe, v_copied, V_USES * tt + before - NC + 1)
                    elif qkv == "b":
                        wait(pe, plain_copied, NC * tt + before + 1)
                    else:
                        wait(pe, rest_ready, NC * tt + before + 1)

                def projections(t, b, half):
                    pe.wait_ge(flip_q_copied, t + 1)
                    flipped_in = flip_q[half % len(flip_q)]
                    for c, (kind, at_c) in enumerate(chunks):
                        bank_free(t, c)
                        rows = P if kind == "q" else KW
                        lhs = (W_Q if kind == "q" else W_K)[:, :, at_c * P:at_c * P + rows]
                        for e in range(EC):
                            mm = nc.tensor.matmul(proj[c % BANKS][0:rows, :], lhs[:, e, :], flipped_in[:, e, :],
                                                  start=(e == 0), stop=(e == EC - 1))
                        mm.then_inc(proj_ready, 1)

                def value_projection(t, b, half):
                    flipped_in = flip_q[half % len(flip_q)]
                    per = SUB // V_USES
                    for use in range(V_USES):
                        bank_free(t, NC + use)
                        bank = proj[(NC + use) % BANKS]
                        for k in range(per):
                            s = use * per + k
                            for e in range(EC):
                                mm = nc.tensor.matmul(bank[:, k * VW:(k + 1) * VW], flipped_in[:, e, s * P:(s + 1) * P],
                                                      W_V[:, e, :], start=(e == 0), stop=(e == EC - 1))
                        mm.then_inc(proj_ready, 1)

                def body(i, n, u):
                    f, q = at("F", i, n, u), at("Q", i, n, u)
                    if "T" not in off:
                        if f:
                            flip_for_ffn(*f)
                        if at("A", i, n, u):
                            out_projection(*at("A", i, n, u))
                        if q:
                            flip_for_qkv(*q, min(q[0] + 2, TILES) if isinstance(i, int) else q[0] + 2)
                        if f:
                            ffn_product(*f)
                        if q:
                            projections(*q)
                            value_projection(*q)
                    elif ffn:
                        if at("A", i, n, u):
                            out_projection(*at("A", i, n, u))
                        if f:
                            ffn_product(*f)
                        if at("T", i, n, u):
                            flip_for_ffn(*at("T", i, n, u))
                    else:
                        if q:
                            projections(*q)
                        if at("T", i, n, u):
                            flip_for_qkv(*at("T", i, n, u))
                        if q:
                            value_projection(*q)

                rounds(pe, body)

            @block.scalar
            def _(act):
                def copy_for_ffn(t, b, half):
                    act.wait_ge(flip_f_ready, t + 1)
                    wait(act, y_ffn_ready, t)
                    nc.scalar.copy(flip_f[:, :, :], flipped[:, :, :]).then_inc(flip_f_copied, 1)

                def copy_for_qkv(t, b, half):
                    act.wait_ge(flip_q_ready, t + 1)
                    wait(act, proj_ready, USES * (t + 1 - len(flip_q)))
                    nc.scalar.copy(flip_q[half % len(flip_q)][:, :, :], flipped[:, :, :]).then_inc(flip_q_copied, 1)

                def high(t, c):
                    rows = P if chunks[c][0] == "q" else KW
                    wait(act, parts_stored[c], 16 * PARTS * t)
                    if qkv == "a":
                        act.wait_ge(proj_ready, USES * t + c + 1)
                        src = proj[c % BANKS]
                    else:
                        act.wait_ge(turned_ready, NC * t + c + 1)
                        src = turned[c]
                    nc.scalar.copy(part[c][0][0:rows, :], src[0:rows, :]).then_inc(high_ready, 1)

                def mid(t, c):
                    rows = P if chunks[c][0] == "q" else KW
                    act.wait_ge(rest_ready, NC * t + c + 1)
                    nc.scalar.copy(part[c][1][0:rows, :], rest[c][0:rows, :]).then_inc(mid_ready, 1)

                def copy_plain(t, c):
                    rows = P if chunks[c][0] == "q" else KW
                    act.wait_ge(proj_ready, USES * t + c + 1)
                    wait(act, swap_ready, NC * (t - 1) + c + 1)
                    wait(act, cos_ready, NC * (t - 1) + c + 1)
                    nc.scalar.copy(plain[c][0:rows, :], proj[c % BANKS][0:rows, :]).then_inc(plain_copied, 1)

                def values(t):
                    per = SUB // V_USES
                    wait(act, v_stored, 16 * NG * t)
                    for use in range(V_USES):
                        act.wait_ge(proj_ready, USES * t + NC + use + 1)
                        src = proj[(NC + use) % BANKS][:, 0:per * VW].rearrange("p (s g v) -> p s g v", s=per, g=NG)
                        for s in range(per):
                            ins = nc.scalar.copy(v_tile[:, :, use * per + s, :], src[:, s, :, :])
                        ins.then_inc(v_copied, 1)

                def deviation(count):
                    act.wait_ge(ln_step, (2 * SUB + 1) * count + 2 * SUB)
                    nc.scalar.activation(std[:, :], moments[:, :, 1], ACT.Sqrt, bias=const["eps"][:, 0:1])\
                        .then_inc(std_ready, 1)

                def body(i, n, u):
                    f, q, split = at("F", i, n, u), at("Q", i, n, u), at("S", i, n, u)
                    if ffn and at(TURN_F, i, n, u):
                        copy_for_ffn(*at(TURN_F, i, n, u))
                    if split:
                        for c in range(NC - 1):
                            high(split[0], c)
                    if at("A", i, n, u):
                        deviation(norms_before("A", at("A", i, n, u)[0]))
                    if qkv == "b" and q:
                        copy_for_qkv(*q)
                    if split:
                        high(split[0], NC - 1)
                        for c in range(NC - 1):
                            mid(split[0], c)
                    if qkv == "b" and q:
                        copy_plain(q[0], 0)
                    if split:
                        mid(split[0], NC - 1)
                    if qkv == "b" and q:
                        copy_plain(q[0], 1)
                    if qkv and f:
                        deviation(norms_before("F", f[0]))
                    if qkv == "b" and q:
                        copy_plain(q[0], 2)
                    if qkv == "a" and q:
                        for c in range(NC):
                            high(q[0], c)
                            if c:
                                mid(q[0], c - 1)
                    if qkv == "a" and at("T", i, n, u):
                        copy_for_qkv(*at("T", i, n, u))
                    if qkv == "a" and q:
                        mid(q[0], NC - 1)
                    if q:
                        values(q[0])

                rounds(act, body)

            @block.gpsimd
            def _(pool):
                def add_bias(t, b, half):
                    pool.wait_ge(x1_ready, t + 1)
                    wait(pool, x2_ready, t - 1)
                    nc.gpsimd.tensor_tensor(x1_bias[half][:, :, :], x1[half][:, :, :], w["bias"][:, :, :], ALU.add)\
                        .then_inc(x1_bias_ready, 1)

                def turn_pairs(t, c, half):
                    kind, at_c = chunks[c]
                    rows = P if kind == "q" else KW
                    if isinstance(t, int) and t == c == 0:
                        pool.wait_ge(tables_loaded, 64)
                    pool.wait_ge(swap_ready, NC * t + c + 1)
                    nc.gpsimd.tensor_tensor(swapped[c][0:rows, :], swapped[c][0:rows, :],
                                            sin[kind][:, at_c, half * BANK:(half + 1) * BANK], ALU.mult)\
                        .then_inc(turn_step, 1)
                    pool.wait_ge(turn_step, NC * t + c + 1)
                    pool.wait_ge(cos_ready, NC * t + c + 1)
                    nc.gpsimd.tensor_tensor(turned[c][0:rows, :], turned[c][0:rows, :], swapped[c][0:rows, :], ALU.add)\
                        .then_inc(turned_ready, 1)

                def low(t, c):
                    rows = P if chunks[c][0] == "q" else KW
                    pool.wait_ge(mid_ready, NC * t + c + 1)
                    nc.gpsimd.tensor_tensor(part[c][2][0:rows, :], rest[c][0:rows, :], part[c][1][0:rows, :],
                                            ALU.subtract).then_inc(low_ready, 1)

                def body(i, n, u):
                    if ffn and at("A", i, n, u):
                        add_bias(*at("A", i, n, u))
                    if ffn and qkv and at("O", i, n, u):
                        normalise(nc.gpsimd, *at("O", i, n, u))
                    if at(SPLITS, i, n, u):
                        for c in range(NC):
                            low(at(SPLITS, i, n, u)[0], c)
                    if qkv == "b" and at("Q", i, n, u):
                        t, b, half = at("Q", i, n, u)
                        for c in range(NC):
                            turn_pairs(t, c, half)

                rounds(pool, body)

            @block.vector
            def _(dve):
                def layer_norm(dst, src, count, ready):
                    for s in range(SUB):
                        nc.vector.bn_stats(stats[:, s, :], src[:, s, :]).then_inc(ln_step, 1)
                    for s in range(SUB):
                        dve.wait_ge(ln_step, (2 * SUB + 1) * count + s + 1)
                        apart(dve, const["spare"])
                        nc.vector.bn_aggr(moments[:, s, :], stats[:, s, :]).then_inc(ln_step, 1)
                    dve.wait_ge(std_ready, count + 1)
                    nc.vector.reciprocal(rstd[:, :], std[:, :]).then_inc(ln_step, 1)
                    dve.wait_ge(ln_step, (2 * SUB + 1) * (count + 1))
                    for s in range(SUB):
                        ins = nc.vector.tensor_scalar(dst[:, s, :], src[:, s, :], moments[:, s, 0:1], rstd[:, s:s + 1],
                                                      ALU.subtract, ALU.mult)
                    ins.then_inc(ready, 1)

                def reciprocals(t, b, half):
                    dve.wait_ge(sums_loaded[half], (b + 1) * 16)
                    wait(dve, recip_stored[half], b * 16)
                    nc.vector.reciprocal(recip[half][:, :], sums[half][:, :]).then_inc(recip_ready, 1)

                def first_residual(t, b, half, count):
                    dve.wait_ge(x_loaded[half], (b + 1) * 16)
                    if ffn:
                        dve.wait_ge(y_att_ready, t + 1)
                        wait(dve, x1_bias_ready, t - 1)
                        nc.vector.tensor_tensor(x1[half][:, :, :], y_att[:, :, :], x_tile[half][:, :, :], ALU.add)\
                            .then_inc(x1_ready, 1)
                        dve.wait_ge(x1_ready, t + 1)
                        wait(dve, flip_f_ready, t - 1)
                        layer_norm(normed[half], x1[half], count, ln_a_ready)
                    else:
                        wait(dve, flip_q_ready, t - 1)
                        layer_norm(normed[half], x_tile[half], count, ln_a_ready)

                def second_residual(t, b, half, count):
                    dve.wait_ge(y_ffn_ready, t + 1)
                    dve.wait_ge(x1_bias_ready, t + 1)
                    wait(dve, x2_stored[half], b * 16)
                    nc.vector.tensor_tensor(x2[half][:, :, :], y_ffn[half % len(y_ffn)][:, :, :],
                                            x1_bias[half][:, :, :], ALU.add)\
                        .then_inc(x2_ready, 1)
                    if qkv:
                        dve.wait_ge(x2_ready, t + 1)
                        wait(dve, flip_q_ready, t - 1)
                        layer_norm(ln_f[half], x2[half], count, ln_f_ready)

                def leave(t, c):
                    rows = P if chunks[c][0] == "q" else KW
                    dve.wait_ge(high_ready, NC * t + c + 1)
                    wait(dve, low_ready, NC * (t - 1) + c + 1)
                    src = proj[c % BANKS] if qkv == "a" else turned[c]
                    nc.vector.tensor_tensor(rest[c][0:rows, :], src[0:rows, :], part[c][0][0:rows, :], ALU.subtract)\
                        .then_inc(rest_ready, 1)

                def swap_pairs(t, c, half):
                    kind, at_c = chunks[c]
                    rows = P if kind == "q" else KW
                    if isinstance(t, int) and t == c == 0:
                        dve.wait_ge(tables_loaded, 64)
                    dve.wait_ge(plain_copied, NC * t + c + 1)
                    wait(dve, rest_ready, NC * (t - 1) + c + 1)
                    wait(dve, turned_ready, NC * (t - 1) + c + 1)
                    apart(dve, const["spare"])
                    nc.vector.stream_shuffle(swapped[c][0:rows, :], plain[c][0:rows, :], [r ^ 1 for r in range(32)])\
                        .then_inc(swap_ready, 1)
                    nc.vector.tensor_tensor(turned[c][0:rows, :], plain[c][0:rows, :],
                                            cos[kind][:, at_c, half * BANK:(half + 1) * BANK], ALU.mult)\
                        .then_inc(cos_ready, 1)

                def body(i, n, u):
                    if at("R", i, n, u):
                        reciprocals(*at("R", i, n, u))
                    if ffn and not qkv and at("O", i, n, u):
                        normalise(nc.vector, *at("O", i, n, u))
                    if at("A", i, n, u):
                        first_residual(*at("A", i, n, u), norms_before("A", at("A", i, n, u)[0]))
                    if qkv == "b" and at("S", i, n, u):
                        for c in range(NC):
                            leave(at("S", i, n, u)[0], c)
                    if at("F", i, n, u):
                        second_residual(*at("F", i, n, u), norms_before("F", at("F", i, n, u)[0]))
                    if at("Q", i, n, u):
                        t, b, half = at("Q", i, n, u)
                        for c in range(NC):
                            if qkv == "b":
                                swap_pairs(t, c, half)
                            else:
                                leave(t, c)

                rounds(dve, body)


def attention_phase(nc, tag, const, q_scr, k_scr, v_scr, out_scr, causal, shared_kv, scale):
    KH = 1 if shared_kv else G
    KROWS = NG * KH * D
    LOADS = 2 * len(Q_PARTS)
    ST = SM = 3

    def seen_by(i):
        return (P * i if causal else 0), T

    def cuts(lo, hi, width):
        return [(max(lo, k), min(hi, k + width)) for k in range(0, T, width) if max(lo, k) < min(hi, k + width)]

    UNITS = [(j, i, lo, hi) for j in range(G) for i in range(NT)
             for lo, hi in cuts(0, P * (i + 1) if causal else T, BANK)]
    U = len(UNITS)
    STEPS = [(i, NT - 1 - i) for i in range(NT // 2)] if causal else [(i,) for i in range(NT)]
    NS = len(STEPS)
    START = {i: sum(T - seen_by(before)[0] for before in tiles[:k]) for tiles in STEPS for k, i in enumerate(tiles)}
    WIDTH = sum(T - seen_by(i)[0] for i in STEPS[0])
    TURNS = [(s, j, i, lo, hi) for s in range(NS) for j in range(G) for i in STEPS[s]
             for lo, hi in cuts(*seen_by(i), BANK)]
    S = len(TURNS)
    PIECES = [[(i, lo, hi) for i in STEPS[s] for lo, hi in cuts(*seen_by(i), BANK // 2)] for s in range(NS)]
    NP = len(PIECES[0])
    V = NS * NP
    LAG = 3
    PIECE_AFTER = {(s * S // NS + S // NS + LAG + k * (S // NS) // NP): (s, k) for s in range(NS) for k in range(NP)}
    COMPLETES = [max(k for k, (i, lo, hi) in enumerate(PIECES[NS - 1]) if lo // BANK == bank) for bank in range(2)]
    COPY_AFTER = [next(n for n, piece in PIECE_AFTER.items() if piece == (NS - 1, k)) - S + 1 for k in COMPLETES]
    HEAD_START = U // 3

    def buffer(i, lo, hi):
        return START[i] + lo - seen_by(i)[0], START[i] + hi - seen_by(i)[0]

    def turn_of(i, j, hi):
        return max(n for n, turn in enumerate(TURNS) if turn[1:3] == (j, i) and turn[3] < hi) + 1

    def use_free(banks, n, total):
        return banks if n == 0 and total % banks else 1

    def spread():
        cost = []
        for n, (s, j, i, lo, hi) in enumerate(TURNS):
            s, k = PIECE_AFTER.get(n, PIECE_AFTER.get(n + S, (0, None)))
            width = 0 if k is None else PIECES[s][k][2] - PIECES[s][k][1]
            cost.append(hi - lo + 2.2 * width)
        return [round(U * sum(cost[:n + 1]) / sum(cost)) for n in range(S)]

    QUOTA = spread()

    with ExitStack() as ctx:
        sb = lambda name, shape, dt=F32: ctx.enter_context(nc.sbuf_tensor(tag + name, shape, dt))
        ps = lambda name, shape: ctx.enter_context(nc.psum_tensor(tag + name, shape, F32))
        sem = lambda name: ctx.enter_context(nc.semaphore(tag + name))

        q_ops = [sb(f"q_ops{g}", [ROWS, G, T], BF16) for g in range(NG)]
        k_ops = [sb(f"k_ops{g}", [ROWS, KH, T], BF16) for g in range(NG)]
        v_in = [sb(f"v_in{g}", [P, NT, KH, D]) for g in range(NG)]
        v_ones = [sb(f"v_ones{g}", [P, NT, KH, 2 * D]) for g in range(NG)]
        probs = [sb(f"probs{k}", [P, G, WIDTH]) for k in range(2)]
        out_tile = [sb(f"out_tile{k}", [P, T]) for k in range(2)]
        bank_max = sb("bank_max", [P, 2, G, NT])
        row_max = sb("row_max", [P, G, NT])
        max_parts = sb("max_parts", [P, 2, G * NT], BF16)
        max_turned = [sb(f"max_turned{k}", [P, 2, G * NT], BF16) for k in range(2)]
        scores_t = [ps(f"scores_t{k}", [P, BANK]) for k in range(ST)]
        out_acc = ps("out_acc", [P, T])
        scores = [ps(f"scores{k}", [P, BANK]) for k in range(SM)]

        qk_loaded = [sem(f"qk_loaded{g}") for g in range(NG)]
        v_loaded = [sem(f"v_loaded{g}") for g in range(NG)]
        max_loaded = [sem(f"max_loaded{g}") for g in range(NG)]
        const_ready = sem("const_ready")
        v_ready = sem("v_ready")
        if causal:
            hidden = sem("hidden")
            added = [sb(f"added{k}", [P, BANK], BF16) for k in range(SM)]
        scores_ready, scores_free = sem("scores_ready"), sem("scores_free")
        max_step, max_ready = sem("max_step"), sem("max_ready")
        scores_t_ready, probs_ready, probs_free = sem("scores_t_ready"), sem("probs_ready"), sem("probs_free")
        out_copied = sem("out_copied")
        out_stored = [sem(f"out_stored{k}") for k in range(2)]

        with nc.Block() as block:
            @block.sync
            def _(sp):
                def load(b, g):
                    for k in range(len(Q_PARTS)):
                        src = q_scr[bass.ds((b * PARTS + Q_PARTS[k]) * E + g * G * D, G * D), :]
                        sp.dma_start(q_ops[g][D * k:D * (k + 1), :, :], src.rearrange("(j d) t -> d j t", d=D))\
                            .then_inc(qk_loaded[g], 16)
                        src = k_scr[bass.ds((b * PARTS + K_PARTS[k]) * KROWS + g * KH * D, KH * D), :]
                        sp.dma_start(k_ops[g][D * k:D * (k + 1), :, :], src.rearrange("(j d) t -> d j t", d=D))\
                            .then_inc(qk_loaded[g], 16)

                def load_v(b, g):
                    sp.dma_start(v_in[g][:, :, :, :].rearrange("p i j d -> p (i j d)"),
                                 v_scr[bass.ds((b * NG + g) * P, P), 0:NT * KH * D]).then_inc(v_loaded[g], 16)

                def place_max(b, g):
                    group = b * NG + g
                    sp.wait_ge(max_ready, group + 1)
                    apart(sp, const["spare"])
                    for k in range(2):
                        for a in range(4):
                            dst = q_ops[g][SPLIT + k:SPLIT + k + 1, :, :].rearrange(
                                "o j (i a r) -> o (j i) a r", a=4, r=32)[:, :, a, :]
                            sp.dma_start(dst, max_turned[g % 2][32 * a:32 * a + 32, k, :]).then_inc(max_loaded[g], 16)

                def store(b, g):
                    group = b * NG + g
                    sp.wait_ge(out_copied, 2 * (group + 2))
                    apart(sp, const["spare"])
                    sp.dma_start(out_scr[bass.ds(group * P, P), :], out_tile[g % 2][:, :])\
                        .then_inc(out_stored[g % 2], 16)

                def batch_row(b, last):
                    for g in range(NG):
                        if g + 1 < NG:
                            place_max(b, g + 1)
                        elif not last:
                            place_max(b + 1, 0)
                        if not last:
                            sp.wait_ge(scores_t_ready, S * (b * NG + g + 1))
                            apart(sp, const["spare"])
                            load(b + 1, g)
                            sp.wait_ge(v_ready, b * NG + g + 1)
                            apart(sp, const["spare"])
                            load_v(b + 1, g)
                        store(b, g)

                for k in range(2):
                    sp.sem_inc(out_stored[k], 16)
                for g in range(NG):
                    load(0, g)
                    load_v(0, g)
                place_max(0, 0)
                with sp.Fori(0, BATCH - 1) as b:
                    batch_row(b, False)
                batch_row(BATCH - 1, True)
                for k in range(2):
                    sp.wait_ge(out_stored[k], 16 + 16 * (BATCH * NG // 2))

            @block.gpsimd
            def _(pool):
                for g in range(NG):
                    nc.gpsimd.memset(k_ops[g][SPLIT:ROWS, :, :], -1.0).then_inc(const_ready, 1)
                for g in range(NG):
                    pool.wait_ge(const_ready, NG)
                    nc.gpsimd.memset(v_ones[g][:, :, :, D:2 * D], 1.0).then_inc(const_ready, 1)

                def place_v(b, g, before=None):
                    pool.wait_ge(v_loaded[g], 16 * (b + 1))
                    if before is not None:
                        pool.wait_ge(probs_free, V * (before * NG + g + 2))
                    apart(pool, const["spare"])
                    nc.gpsimd.tensor_copy(v_ones[g][:, :, :, 0:D], v_in[g][:, :, :, :]).then_inc(v_ready, 1)

                def hide_later_keys(b, g, steps):
                    if causal:
                        for s in steps:
                            for j in range(G):
                                for i in STEPS[s]:
                                    pool.wait_ge(probs_ready, S * (b * NG + g) + turn_of(i, j, P * (i + 1)) + ST)
                                    apart(pool, const["spare"])
                                    lo, hi = buffer(i, P * i, P * (i + 1))
                                    diagonal = probs[s % 2][:, j, lo:hi]
                                    nc.gpsimd.affine_select(out=diagonal, in_=diagonal,
                                                            compare_op=ALU.is_ge, fill=0.0, base=0, pattern=[[1, P]],
                                                            channel_multiplier=-1).then_inc(hidden, 1)

                def window(b, g, last):
                    hide_later_keys(b, g, range(NS // 2))
                    if not last:
                        place_v(b if g == 0 else b + 1, (g - 1) % NG, b - 1 if g == 0 else b)
                    hide_later_keys(b, g, range(NS // 2, NS))

                for g in range(NG):
                    place_v(0, g)
                hide_later_keys(0, 0, range(NS))
                with pool.Fori(0, BATCH - 1) as b:
                    for g in range(1, NG):
                        window(b, g, False)
                    window(b + 1, 0, False)
                if causal:
                    for g in range(1, NG):
                        window(BATCH - 1, g, True)

            @block.tensor
            def _(pe):
                pe.sem_inc(probs_free, V)
                def max_unit(b, g, n):
                    j, i, lo, hi = UNITS[n]
                    if n == 0:
                        pe.wait_ge(qk_loaded[g], 16 * LOADS * (b + 1))
                    pe.wait_ge(scores_free, U * (b * NG + g) + n + use_free(SM, g * U + n, NG * U))
                    bank = scores[(g * U + n) % SM]
                    nc.tensor.matmul(bank[:, 0:hi - lo], q_ops[g][0:SPLIT, j, P * i:P * (i + 1)],
                                     k_ops[g][0:SPLIT, j % KH, lo:hi], start=True, stop=True).then_inc(scores_ready, 1)

                def transposed_scores(b, g, n):
                    s, j, i, lo, hi = TURNS[n]
                    pe.wait_ge(probs_ready, S * (b * NG + g) + n + use_free(ST, g * S + n, NG * S))
                    nc.tensor.matmul(scores_t[(g * S + n) % ST][:, 0:hi - lo],
                                     k_ops[g][:, j % KH, P * i:P * (i + 1)], q_ops[g][:, j, lo:hi],
                                     start=True, stop=True).then_inc(scores_t_ready, 1)

                def weigh_values(b, g, s, k):
                    group = b * NG + g
                    i, lo, hi = PIECES[s][k]
                    if s == 0 and k == 0:
                        pe.wait_ge(v_ready, group + 1)
                    if i == 0 and lo % BANK == 0:
                        pe.wait_ge(out_copied, 2 * group + lo // BANK + 1)
                    pe.wait_ge(probs_ready, S * group + turn_of(i, G - 1, hi) + ST)
                    if causal and lo == P * i:
                        tiles = STEPS[s]
                        pe.wait_ge(hidden, len(tiles) * G * (NS * group + s + 1) - len(tiles) + tiles.index(i) + 1)
                    a, z = buffer(i, lo, hi)
                    for j in range(G):
                        mm = nc.tensor.matmul(out_acc[32 * j:32 * j + 32, lo:hi], v_ones[g][:, i, j % KH, :],
                                              probs[s % 2][:, j, a:z], start=(i == 0 and lo % BANK == 0), stop=True,
                                              skip_group_check=True)
                    mm.then_inc(probs_free, 1)

                def window(b, g, before, last=False):
                    pe.wait_ge(max_loaded[g], 16 * 8 * (b + 1))
                    units = []
                    for ahead, ns in ((1, range(HEAD_START, U)), (2, range(HEAD_START))):
                        if not (last and g + ahead >= NG):
                            units += [(b + (g + ahead) // NG, (g + ahead) % NG, n) for n in ns]
                    taken = 0
                    for n in range(S):
                        transposed_scores(b, g, n)
                        while taken < min(QUOTA[n], len(units)):
                            max_unit(*units[taken])
                            taken += 1
                        if n in PIECE_AFTER:
                            weigh_values(b, g, *PIECE_AFTER[n])
                        if before and n + S in PIECE_AFTER:
                            weigh_values(*before, *PIECE_AFTER[n + S])

                for n in range(U):
                    max_unit(0, 0, n)
                for n in range(HEAD_START):
                    max_unit(0, 1, n)
                pe.wait_ge(const_ready, 2 * NG)
                window(0, 0, None)
                nc.disable_value_cache = True
                with pe.Fori(0, BATCH - 1) as b:
                    for g in range(1, NG):
                        window(b, g, (b, g - 1), False)
                    window(b + 1, 0, (b, NG - 1), False)
                nc.disable_value_cache = False
                for g in range(1, NG):
                    window(BATCH - 1, g, (BATCH - 1, g - 1), True)
                for n in range(S, 2 * S):
                    if n in PIECE_AFTER:
                        weigh_values(BATCH - 1, NG - 1, *PIECE_AFTER[n])

            @block.scalar
            def _(act):
                act.sem_inc(probs_ready, ST)
                act.sem_inc(out_copied, 2)

                def copy_out(b, g, bank):
                    group = b * NG + g
                    act.wait_ge(probs_free, V * (group + 1) + NP * (NS - 1) + COMPLETES[bank] + 1)
                    if bank == 0:
                        act.wait_ge(out_stored[g % 2], 16 * (b * NG // 2 + g // 2 + 1))
                    nc.scalar.copy(out_tile[g % 2][:, bank * BANK:(bank + 1) * BANK],
                                   out_acc[:, bank * BANK:(bank + 1) * BANK]).then_inc(out_copied, 1)

                def window(b, g, before):
                    group = b * NG + g
                    for n, (s, j, i, lo, hi) in enumerate(TURNS):
                        a, z = buffer(i, lo, hi)
                        if j == 0:
                            step = (s - 2) % NS
                            used = max(k for k, piece in enumerate(PIECES[step]) if buffer(*piece)[0] < z) + 1
                            act.wait_ge(probs_free, V * (group + (s >= 2)) + NP * step + used)
                        act.wait_ge(scores_t_ready, S * group + n + 1)
                        nc.scalar.activation(probs[s % 2][:, j, a:z], scores_t[(g * S + n) % ST][:, 0:hi - lo],
                                             ACT.Exp, scale=scale).then_inc(probs_ready, 1)
                        if before and n in COPY_AFTER:
                            copy_out(*before, COPY_AFTER.index(n))

                window(0, 0, None)
                with act.Fori(0, BATCH - 1) as b:
                    for g in range(1, NG):
                        window(b, g, (b, g - 1))
                    window(b + 1, 0, (b, NG - 1))
                for g in range(1, NG):
                    window(BATCH - 1, g, (BATCH - 1, g - 1))
                for bank in range(2):
                    copy_out(BATCH - 1, NG - 1, bank)

            @block.vector
            def _(dve):
                dve.sem_inc(scores_free, SM)

                def maxima(b, g):
                    group = b * NG + g
                    for n, (j, i, lo, hi) in enumerate(UNITS):
                        dve.wait_ge(scores_ready, U * group + n + 1)
                        alone = causal and i < BANK // P
                        dst = row_max[:, j, i:i + 1] if alone else bank_max[:, lo // BANK, j, i:i + 1]
                        bank = scores[(g * U + n) % SM][:, 0:hi - lo]
                        if causal and hi == P * (i + 1):
                            apart(dve, const["spare"])
                            ins = nc.vector.tensor_tensor_reduce(added[(g * U + n) % SM][:, 0:hi - lo], bank,
                                                                 const["hide"][:, BANK - (hi - lo):], 1.0, 2 * HIDDEN,
                                                                 ALU.add, ALU.max, dst)
                        else:
                            ins = nc.vector.tensor_reduce(dst, bank, AX.X, ALU.max)
                        ins.then_inc(scores_free, 1)
                    dve.wait_ge(scores_free, U * (group + 1) + SM)
                    i0 = BANK // P if causal else 0
                    nc.vector.tensor_tensor(row_max[:, :, i0:NT], bank_max[:, 0, :, i0:NT], bank_max[:, 1, :, i0:NT],
                                            ALU.max).then_inc(max_step, 1)
                    dve.wait_ge(max_step, 3 * group + 1)
                    nc.vector.tensor_copy(max_parts[:, 0, :], row_max[:, :, :].rearrange("p j i -> p (j i)"))\
                        .then_inc(max_step, 1)
                    dve.wait_ge(max_step, 3 * group + 2)
                    nc.vector.tensor_tensor(max_parts[:, 1, :], row_max[:, :, :].rearrange("p j i -> p (j i)"),
                                            max_parts[:, 0, :], ALU.subtract).then_inc(max_step, 1)
                    dve.wait_ge(max_step, 3 * group + 3)
                    nc.vector.transpose(max_turned[g % 2][:, :, :].rearrange("p k c -> p (k c)"),
                                        max_parts[:, :, :].rearrange("p k c -> p (k c)")).then_inc(max_ready, 1)

                with dve.Fori(0, BATCH) as b:
                    for g in range(NG):
                        maxima(b, g)


def build(nc, x, qkvT, outT, q_b, k_b, v_b, out_b, ffn, bias, lora_aT, lora_b, cos_q, sin_q, cos_k, sin_k, out):
    scr = lambda name, shape, dt=F32: nc.dram_tensor(name, shape, dt, kind="Internal").ap()
    x_rows = x.rearrange("b t e -> (b t) e")
    out_rows = out.rearrange("b t e -> (b t) e")
    q_scr = [scr(f"q_parts_{l}", [BATCH * PARTS * E, T], BF16) for l in "ab"]
    k_scr = [scr("k_parts_a", [BATCH * PARTS * E, T], BF16), scr("k_parts_b", [BATCH * PARTS * E // G, T], BF16)]
    v_scr = [scr("v_a", [BATCH * NG * P, NT * G * D]), scr("v_b", [BATCH * NG * P, NT * D])]
    att_scr = [scr(f"attended_{l}", [BATCH * NG * P, T]) for l in "ab"]
    recip_scr = [scr(f"recip_{l}", [BATCH * H, T]) for l in "ab"]
    x_mid = scr("x_mid", [BATCH * T, E])

    with ExitStack() as ctx:
        sb = lambda name, shape, dt=F32: ctx.enter_context(nc.sbuf_tensor(name, shape, dt))
        w = {"qkvT": sb("w_qkvT", [P, EC, 3 * E]), "outT": sb("w_outT", [P, EC, E]), "q_b": sb("w_q_b", [P, EC, E]),
             "k_b": sb("w_k_b", [P, EC, E // G]), "v_b": sb("w_v_b", [P, EC, E // G]),
             "out_b": sb("w_out_b", [P, EC, E]),
             "ffn": sb("w_ffn", [P, EC, E]), "bias": sb("w_bias", [P, SUB, E])}
        const = {"spare": ctx.enter_context(nc.semaphore("spare")), "eps": sb("eps", [P, 1]),
                 "ident": sb("ident", [P, P]),
                 "hide": sb("hide", [P, BANK], BF16)}
        src = {"qkvT": qkvT, "outT": outT, "q_b": q_b, "k_b": k_b, "v_b": v_b, "out_b": out_b, "ffn": ffn,
               "bias": bias, "lora_aT": lora_aT, "lora_b": lora_b}
        tables = {"cos_q": cos_q, "sin_q": sin_q, "cos_k": cos_k, "sin_k": sin_k}
        weights_phase(nc, src, w, const)
        token_phase(nc, "t1_", w, const, x_rows, None, None, None, None, "a", q_scr[0], k_scr[0], v_scr[0], None)
        attention_phase(nc, "a_", const, q_scr[0], k_scr[0], v_scr[0], att_scr[0], causal=True, shared_kv=False,
                        scale=float(D) ** -0.5)
        token_phase(nc, "t2_", w, const, x_rows, x_mid, att_scr[0], recip_scr[0], w["outT"], "b",
                    q_scr[1], k_scr[1], v_scr[1], tables)
        attention_phase(nc, "b_", const, q_scr[1], k_scr[1], v_scr[1], att_scr[1], causal=False, shared_kv=True,
                        scale=float(E) ** -0.5)
        token_phase(nc, "t3_", w, const, x_mid, out_rows, att_scr[1], recip_scr[1], w["out_b"], None,
                    None, None, None, None)


def rope_tables():
    f = np.float32
    inv = (f(1.0) / (f(10000.0) ** (np.arange(0, E, 2, dtype=f) / f(E)))).astype(f)
    ang = (np.arange(T, dtype=f)[None, :] * inv[:, None]).astype(f)
    cos, sin = np.cos(ang).astype(f), np.sin(ang).astype(f)
    wide = lambda a: np.repeat(a, 2, axis=0)
    signs = lambda a: np.stack([-a, a], axis=1).reshape(-1, a.shape[1])
    heads = lambda a: np.concatenate([a] * NG, axis=0)
    half = D // 2
    return {"cos_q": wide(cos), "sin_q": signs(sin),
            "cos_k": heads(wide(cos[:half])), "sin_k": heads(signs(sin[:half]))}


def kernel(**inputs):
    import concourse.bacc as bacc
    from concourse.bass_utils import run_bass_kernel_spmd

    a = {k: np.asarray(v) for k, v in inputs.items()}
    arrays = {
        "x": a["L0_attn_a_x"], "qkvT": a["L0_attn_a_W_qkv"].T, "outT": a["L0_attn_a_W_out"].T,
        "q_b": a["L0_attn_b_Wq"], "k_b": a["L0_attn_b_Wk"], "v_b": a["L0_attn_b_Wv"], "out_b": a["L0_attn_b_Wo"],
        "ffn": a["L0_ffn_kernel"], "bias": a["L0_ffn_bias"], "lora_aT": a["L0_ffn_a"].T, "lora_b": a["L0_ffn_b"],
        **rope_tables(),
    }
    nc = bacc.Bacc("TRN2", target_bir_lowering=False, num_devices=1)
    maps, args = {}, []
    for name, value in arrays.items():
        value = np.ascontiguousarray(value)
        maps[f"in_{name}"] = value
        args.append(nc.dram_tensor(f"in_{name}", value.shape, mybir.dt.from_np(value.dtype), kind="ExternalInput").ap())
    out = nc.dram_tensor("out_x", (BATCH, T, E), F32, kind="ExternalOutput").ap()
    build(nc, *args, out)
    result = run_bass_kernel_spmd(nc, [maps], core_ids=[0])
    return result.results[0]["out_x"]
```
